# Optimizing a Trainium2 kernel written in Bass

```python
import numpy as np
import jax
import jax.numpy as jnp

def _softmax(x, axis=-1):
    return jax.nn.softmax(x, axis=axis)

def _gelu(x):
    return jax.nn.gelu(x, approximate=True)

def _silu(x):
    return jax.nn.silu(x)

def _sigmoid(x):
    return jax.nn.sigmoid(x)

def _layernorm(x, axis=-1, eps=1e-05):
    m = jnp.mean(x, axis=axis, keepdims=True)
    v = jnp.var(x, axis=axis, keepdims=True)
    return (x - m) / jnp.sqrt(v + eps)

def _scatter_add(tgt, idx, src, axis=0):
    return tgt.at[idx].add(src)

def _segment_sum(src, seg, n):
    return jax.ops.segment_sum(src, seg, n)
kernel_name = 'mk_adj_preln_d1_adj_r2_b501fa'

def setup_inputs(seed: int=0):
    np.random.seed(seed)
    _w = jnp.asarray

    def _rec_inputs():
        import jax
        import jax.numpy as jnp
        _gk = jax.random.key(seed)
        x = 7.22e-05 + 1 * jax.random.normal(jax.random.fold_in(_gk, 1), (4096, 512), jnp.float32)
        _w = (1.0 + jnp.arange(4096, dtype=jnp.float32)) ** (-0.5)
        _w = _w / _w.mean()
        _pij = jnp.clip(0.000488281 * _w[:, None] * _w[None, :], 0.0, 1.0)
        _a = jax.random.uniform(jax.random.fold_in(_gk, 2), (4096, 4096)) < _pij
        _af = _a.astype(jnp.float32)
        adj = _af
        return (x, adj)
    x, adj = _rec_inputs()

    def _L0_gnn_setup():
        import jax, jax.numpy as jnp
        import numpy as np
        N = 4096
        D = 512
        key = jax.random.key(seed)
        ks = jax.random.split(key, 13)
        w_scale = 1.0 / np.sqrt(D)
        inp = {'query': jax.random.normal(ks[0], (N, D), dtype=jnp.float32), 'key': jax.random.normal(ks[1], (N, D), dtype=jnp.float32), 'value': jax.random.normal(ks[2], (N, D), dtype=jnp.float32), 'adj_matrix': jax.random.randint(ks[3], (N, N), 0, 2).astype(jnp.float32), 'Wq': jax.random.normal(ks[4], (D, D), dtype=jnp.float32) * w_scale, 'bq': jax.random.normal(ks[5], (D,), dtype=jnp.float32) * 0.01, 'Wk': jax.random.normal(ks[6], (D, D), dtype=jnp.float32) * w_scale, 'bk': jax.random.normal(ks[7], (D,), dtype=jnp.float32) * 0.01, 'Wv': jax.random.normal(ks[8], (D, D), dtype=jnp.float32) * w_scale, 'bv': jax.random.normal(ks[9], (D,), dtype=jnp.float32) * 0.01, 'Wm': jax.random.normal(ks[10], (D, D), dtype=jnp.float32) * w_scale, 'bm': jax.random.normal(ks[11], (D,), dtype=jnp.float32) * 0.01}
        return inp
    _L0_gnn_all = _L0_gnn_setup()
    _L0_gnn_in = {k: v for k, v in _L0_gnn_all.items() if k in ('key', 'value', 'Wq', 'bq', 'Wk', 'bk', 'Wv', 'bv', 'Wm', 'bm')}
    del _L0_gnn_all
    return {'x': x, 'adj': adj, 'L0_gnn_key': _L0_gnn_in['key'], 'L0_gnn_value': _L0_gnn_in['value'], 'L0_gnn_Wq': _L0_gnn_in['Wq'], 'L0_gnn_bq': _L0_gnn_in['bq'], 'L0_gnn_Wk': _L0_gnn_in['Wk'], 'L0_gnn_bk': _L0_gnn_in['bk'], 'L0_gnn_Wv': _L0_gnn_in['Wv'], 'L0_gnn_bv': _L0_gnn_in['bv'], 'L0_gnn_Wm': _L0_gnn_in['Wm'], 'L0_gnn_bm': _L0_gnn_in['bm']}

def reference(x, adj, L0_gnn_key, L0_gnn_value, L0_gnn_Wq, L0_gnn_bq, L0_gnn_Wk, L0_gnn_bk, L0_gnn_Wv, L0_gnn_bv, L0_gnn_Wm, L0_gnn_bm):
    import jax
    import jax.numpy as jnp

    def _L0_gnn_ref(query, key, value, adj_matrix, Wq, bq, Wk, bk, Wv, bv, Wm, bm):
        import jax, jax.numpy as jnp
        import numpy as np
        N = 4096
        D = 512
        q = query @ Wq.T + bq
        k = key @ Wk.T + bk
        v = value @ Wv.T + bv
        scale = q.shape[0] ** 0.5
        scores = jnp.einsum('nd,md->nm', q, k) / scale
        adj_scores = scores * adj_matrix
        adj_scores = jnp.where(jnp.abs(adj_scores) < 1e-05, -1000000000.0, adj_scores)
        prob = jax.nn.softmax(adj_scores, axis=-1)
        x = jnp.einsum('nm,md->nd', prob, v)
        return x @ Wm.T + bm
    h = jnp.maximum(_layernorm(x, axis=-1), 0.0)
    x = x + _L0_gnn_ref(h, L0_gnn_key, L0_gnn_value, adj, L0_gnn_Wq, L0_gnn_bq, L0_gnn_Wk, L0_gnn_bk, L0_gnn_Wv, L0_gnn_bv, L0_gnn_Wm, L0_gnn_bm)
    return x

_drawn_inputs = setup_inputs


def setup_inputs(seed=0):
    import zlib

    import numpy as np

    out = dict(_drawn_inputs(seed))
    spreads = {}
    factors = {'L0_gnn_bq': 62.074, 'L0_gnn_bk': 64.0, 'L0_gnn_bv': 7.201, 'L0_gnn_bm': 6.729}
    for name, (base, spread) in spreads.items():
        noise = np.random.default_rng([zlib.crc32(name.encode()), seed]).standard_normal(out[name].shape)
        drawn = base * np.exp(spread * noise) if base else spread * noise
        out[name] = jnp.asarray(drawn.astype(out[name].dtype))
    for name, factor in factors.items():
        out[name] = (out[name] * factor).astype(out[name].dtype)
    return out
```

```python
import concourse.bass as bass
from concourse import mybir
from contextlib import ExitStack


def adjacency_attention(
    nc: bass.Bass,
    x: bass.AP,
    adj: bass.AP,
    key: bass.AP,
    value: bass.AP,
    Wq: bass.AP,
    bq: bass.AP,
    Wk: bass.AP,
    bk: bass.AP,
    Wv: bass.AP,
    bv: bass.AP,
    Wm: bass.AP,
    bm: bass.AP,
    out: bass.AP,
):
    fp32 = mybir.dt.float32
    fp16 = mybir.dt.float16
    i32 = mybir.dt.int32
    ALU = mybir.AluOpType
    ACT = mybir.ActivationFunctionType
    AX = mybir.AxisListType

    N, D = x.shape
    P = 128
    NT = N // P
    DT = D // P
    NC = N // 512
    CT = 512 // P
    NS = NT // CT
    EPS = 1e-5
    LIMIT = 1e-5
    MASKED = -1e9
    INV_ROOT = 1.0 / float(N) ** 0.5
    TOP = 2.0 ** 14
    PSCALE = 2.0 ** 14
    HLAG = 10
    VLAG = 11

    q_scratch = nc.dram_tensor("q_scratch", [NT, P, DT, 2, P], fp16, kind="Internal").ap()

    ctx = ExitStack()
    with ctx:
        def sb(name, shape, dt=fp32):
            return ctx.enter_context(nc.sbuf_tensor(name, shape, dt))

        def sem(name):
            return ctx.enter_context(nc.semaphore(name))

        key_sb = sb("key_sb", [P, NT, D])
        v_sb = sb("v_sb", [P, NT + 1, D])
        k16 = key_sb[:, :, :].bitcast(fp16).rearrange("p t (h f m) -> p t h f m", h=2, f=DT)
        v16 = v_sb[:, :, :].bitcast(fp16).rearrange("p t (h d) -> p t h d", h=2)
        arena = sb("arena", [P, 16 * 1024])
        ident = sb("ident", [P, P])
        ones = sb("ones", [P, P])
        out_bias = sb("out_bias", [P, D])
        wq_bk = sb("wq_bk", [P, D])
        scrap = sb("scrap", [P, D])
        bm_row = sb("bm_row", [1, D])
        b_cols = sb("b_cols", [P, 3, DT])
        q_bias = sb("q_bias", [P, DT])
        c_all = sb("c_all", [P, NT])
        c_cur = sb("c_cur", [P, 2])
        bq_bk = sb("bq_bk", [P, 1])
        kmax = sb("kmax", [P, NT])
        vmax = sb("vmax", [P, NT])
        kv_max = sb("kv_max", [P, 2])
        kv_row = sb("kv_row", [1, 2])
        top3 = sb("top3", [P, 3])
        pow3 = sb("pow3", [P, 3])
        rec3 = sb("rec3", [P, 3])
        scale3 = sb("scale3", [P, 3])
        inv3 = sb("inv3", [P, 3])
        q_sq = sb("q_sq", [P, 4])
        inv_qk = sb("inv_qk", [P, 1])
        inv_qk0 = sb("inv_qk0", [P, 1])
        inv_pv = sb("inv_pv", [P, 1])
        stats = sb("stats", [P, CT, 6])
        meanvar = sb("meanvar", [P, CT, 2])
        ln = sb("ln", [P, 6, CT])
        c_raw = sb("c_raw", [P, CT])
        chunk_max = sb("chunk_max", [P, NC])
        neg_max = sb("neg_max", [P, 2])
        den = sb("den", [P, 2])
        rden = sb("rden", [P, 2])

        def kib(at, size, shape=None, **dims):
            view = arena[:, at * 256:(at + size) * 256]
            return view.rearrange(shape, **dims) if shape else view

        wq_sb = kib(0, 8, "p (t n) -> p t n", t=DT)
        wk_sb = kib(8, 8, "p (t n) -> p t n", t=DT)
        wv_sb = kib(16, 8, "p (t n) -> p t n", t=DT)
        wm_sb = kib(24, 8, "p (t n) -> p t n", t=DT)
        wmT = kib(40, 8, "p (t n) -> p t n", t=DT)
        vproj = kib(32, 8, "p (t n) -> p t n", t=DT)
        a_sb = kib(16, 8, "p (t n) -> p t n", t=DT)
        b_rep = kib(48, 6, "p (b t n) -> p b t n", b=3, t=DT)
        a_sq = kib(56, 8, "p (t n) -> p t n", t=DT)
        val_in = kib(24, 8, "p (s n) -> p s n", s=4)
        valT = kib(40, 4, "p (s n) -> p s n", s=2)
        x_in = [kib(24, 8, "p (r n) -> p r n", r=CT), kib(56, 8, "p (r n) -> p r n", r=CT)]
        hT = [kib(0, 8, "p (f n) -> p f n", f=DT), kib(8, 8, "p (f n) -> p f n", f=DT)]
        qT_f32 = kib(44, 4, "p (s n) -> p s n", s=2)
        q_stage = kib(48, 8).bitcast(fp16).rearrange("p (r f h n) -> p r f h n", r=CT, f=DT, h=2)
        probs = [kib(0, 16), kib(16, 16)]
        adj_half = [kib(32, 8), kib(40, 8)]
        pT = kib(48, 4).bitcast(fp16).rearrange("p (s h n) -> p s h n", s=2, h=2)
        qT = kib(52, 4).bitcast(fp16).rearrange("p (s f h n) -> p s f h n", s=2, f=DT, h=2)
        x_row = kib(56, 4, "p (s n) -> p s n", s=2)
        o_row = kib(60, 4, "p (s n) -> p s n", s=2)

        bank = [ctx.enter_context(nc.psum_tensor(f"bank{i}", [P, 512], fp32)) for i in range(8)]

        s_wm, s_wv, s_wq, s_wk, s_b = (sem(n) for n in ("s_wm", "s_wv", "s_wq", "s_wk", "s_b"))
        s_bm = sem("s_bm")
        s_id0 = sem("s_id0")
        s_const = sem("s_const")
        s_rep = sem("s_rep")
        s_wmT_ps = sem("s_wmT_ps")
        s_wmT = sem("s_wmT")
        s_vproj_ps = sem("s_vproj_ps")
        s_vproj = sem("s_vproj")
        s_a_ps = sem("s_a_ps")
        s_a = sem("s_a")
        s_asq = sem("s_asq")
        s_rows_ps = sem("s_rows_ps")
        s_rows = sem("s_rows")
        s_norm_ps = sem("s_norm_ps")
        s_bound2 = sem("s_bound2")
        s_bound = sem("s_bound")
        s_val = [sem(f"s_val{i}") for i in range(4)]
        s_key = [sem(f"s_key{i}") for i in range(4)]
        s_vtr = sem("s_vtr")
        s_valT = sem("s_valT")
        s_vmm = sem("s_vmm")
        s_v = sem("s_v")
        s_kread = sem("s_kread")
        s_vmax = sem("s_vmax")
        s_kvmax = sem("s_kvmax")
        s_kvT = sem("s_kvT")
        s_kvrow = sem("s_kvrow")
        s_kvall = sem("s_kvall")
        s_scales = sem("s_scales")
        s_dve = sem("s_dve")
        s_x = [sem(f"s_x{i}") for i in range(2)]
        s_var = sem("s_var")
        s_sqrt = sem("s_sqrt")
        s_lnc = sem("s_lnc")
        s_ln = [sem(f"s_ln{i}") for i in range(7)]
        s_scrap = sem("s_scrap")
        s_h = sem("s_h")
        s_c = sem("s_c")
        s_hT_ps = sem("s_hT_ps")
        s_hT = sem("s_hT")
        s_q_ps = sem("s_q_ps")
        s_q32 = sem("s_q32")
        s_qhi = sem("s_qhi")
        s_qlo = sem("s_qlo")
        s_qout = sem("s_qout")
        s_kT_ps = sem("s_kT_ps")
        s_khi = sem("s_khi")
        s_klo = sem("s_klo")
        s_vhi = sem("s_vhi")
        s_vlo = sem("s_vlo")
        s_adj = [sem(f"s_adj{i}") for i in range(2)]
        s_qT = [sem(f"s_qT{i}") for i in range(2)]
        s_xrow = [sem(f"s_xrow{i}") for i in range(2)]
        s_xb = sem("s_xb")
        s_ccur = sem("s_ccur")
        s_qk = sem("s_qk")
        s_score = sem("s_score")
        s_times = sem("s_times")
        s_abs = sem("s_abs")
        s_mask = sem("s_mask")
        s_masked = sem("s_masked")
        s_nmax = sem("s_nmax")
        s_exp = sem("s_exp")
        s_tr = sem("s_tr")
        s_phi = sem("s_phi")
        s_plo = sem("s_plo")
        s_pv = sem("s_pv")
        s_rd = sem("s_rd")
        s_rden = sem("s_rden")
        s_fin = sem("s_fin")
        s_out = [sem(f"s_out{i}") for i in range(2)]

        x_t = x.rearrange("(t p) d -> t p d", p=P)
        x_s = x.rearrange("(s r p) d -> s p r d", p=P, r=CT)
        key_t = key.rearrange("(t p) d -> t p d", p=P)
        val_t = value.rearrange("(t p) d -> t p d", p=P)
        adj_t = adj.rearrange("(t p) (h m) -> t h p m", p=P, h=2)
        out_t = out.rearrange("(t p) d -> t p d", p=P)

        def row(view, b):
            if isinstance(b, int):
                return view[b]
            rest = " ".join("bcdef"[:len(view.shape) - 2])
            return view[bass.ds(b, 1)].rearrange(f"o a {rest} -> (o a) {rest}")

        def col(view, b, n=1):
            return view[:, b:b + n] if isinstance(b, int) else view[:, bass.ds(b, n)]

        def tile_of(tensor, t):
            if isinstance(t, int):
                return tensor[:, t, :]
            return tensor[:, bass.ds(t, 1), :].rearrange("p o n -> p (o n)")

        def half_of(tensor, t, h):
            view = tensor[:, :, :].bitcast(fp16)
            if isinstance(t, int):
                return view[:, t, h * D:(h + 1) * D]
            return view[:, bass.ds(t, 1), h * D:(h + 1) * D].rearrange("p o n -> p (o n)")

        def value_phase(eng, tile):
            for r in range(4):
                tile(r, r, False)
            with eng.Fori(4, NT - 7, 4) as t:
                for r in range(4):
                    tile(t + r, r, False)
            for r in range(4):
                tile(NT - 4 + r, r, r == 3)

        def q_phase(eng, prepare, project):
            prepare(0, 0)
            prepare(1, 1)
            project(0, 0)
            with eng.Fori(1, NS - 2, 2) as s:
                prepare(s + 1, 0)
                project(s, 1)
                prepare(s + 2, 1)
                project(s + 1, 0)
            project(NS - 1, 1)

        def main_phase(eng, block):
            for b in range(4):
                block(b, b % 2)
            with eng.Fori(4, NT - 1, 2) as b:
                block(b, 0)
                block(b + 1, 1)
            block(NT, 0)
            block(NT + 1, 1)

        def lagged(b, c, lag):
            back = (lag - c + NC - 1) // NC if lag > c else 0
            blk, chunk = b - back, c - lag + back * NC
            if isinstance(b, int) and not 0 <= blk < NT:
                return None
            return blk, chunk, back

        block_ = ctx.enter_context(nc.Block())

        @block_.sync
        def _(sp):
            sp.dma_start(wm_sb, Wm.rearrange("(t p) n -> p t n", p=P)).then_inc(s_wm, 16)
            sp.dma_start(wv_sb, Wv.rearrange("(t p) n -> p t n", p=P)).then_inc(s_wv, 16)
            for i, b in enumerate((bq, bk)):
                sp.dma_start(b_cols[:, i, :], b.rearrange("(p t) -> p t", p=P)).then_inc(s_b, 16)
            sp.dma_start(b_cols[:, 2, :], bv.rearrange("(t p) -> p t", p=P), allow_slow_non_contiguous=True).then_inc(s_b, 16)
            sp.dma_start(bm_row[:, :], bm.rearrange("(o n) -> o n", o=1)).then_inc(s_bm, 16)
            sp.dma_start(wq_sb, Wq.rearrange("(p t) n -> p t n", p=P)).then_inc(s_wq, 16)
            sp.dma_start(wk_sb, Wk.rearrange("(p t) n -> p t n", p=P)).then_inc(s_wk, 16)
            sp.wait_ge(s_wmT_ps, DT)

            def load_tile(t, r, last):
                if not (isinstance(t, int) and t < 4):
                    sp.wait_ge(s_vtr, t - 3)
                sp.dma_start(val_in[:, r, :], row(val_t, t)).then_inc(s_val[r], 16)
                if not (isinstance(t, int) and t < 4):
                    sp.wait_ge(s_kread, t - 3)
                sp.dma_start(tile_of(key_sb, t), row(key_t, t)).then_inc(s_key[r], 16)

            value_phase(sp, load_tile)
            sp.wait_ge(s_vtr, NT)

            def load_x(s, par):
                if isinstance(s, int) and s == 1:
                    sp.wait_ge(s_norm_ps, 1)
                if not (isinstance(s, int) and s < 2):
                    sp.wait_ge(s_hT_ps, DT * (s - 1))
                    sp.wait_ge(s_c, s - 1)
                sp.dma_start(x_in[par], row(x_s, s)).then_inc(s_x[par], 16)

            def store_q(s, par):
                sp.wait_ge(s_qlo, DT * (s + 1))
                dst = q_scratch.rearrange("(s r) p f h n -> s p r (f h n)", r=CT)
                sp.dma_start(row(dst, s), q_stage.rearrange("p r f h n -> p r (f h n)")).then_inc(s_qout, 16)

            q_phase(sp, load_x, store_q)
            sp.wait_ge(s_qout, 16 * NS)
            sp.wait_ge(s_hT_ps, DT * NS)
            sp.wait_ge(s_c, NS)
            sp.wait_ge(s_q_ps, DT * NS)
            sp.wait_ge(s_qlo, DT * NS)

            def block(b, par):
                if not (isinstance(b, int) and b >= NT):
                    load(b, par)
                if not (isinstance(b, int) and b < 2):
                    sp.wait_ge(s_fin, b - 1)
                    sp.dma_start(row(out_t, b - 2), o_row[:, par, :]).then_inc(s_out[par], 16)

            def load(b, par):
                if not (isinstance(b, int) and b < 2):
                    sp.wait_ge(s_qk, NC * (b - 1))
                sp.dma_start(qT[:, par].rearrange("p f h n -> p (f h n)"),
                             row(q_scratch, b).rearrange("p f h n -> p (f h n)")).then_inc(s_qT[par], 16)
                for h in range(2):
                    if not (isinstance(b, int) and b < 1):
                        sp.wait_ge(s_masked, NC * (b - 1) + 4 * h + 4)
                    sp.dma_start(adj_half[h], row(adj_t[:, h], b)).then_inc(s_adj[h], 16)
                if not (isinstance(b, int) and b < 2):
                    sp.wait_ge(s_fin, b - 1)
                sp.dma_start(x_row[:, par, :], row(x_t, b)).then_inc(s_xrow[par], 16)

            main_phase(sp, block)
            for par in range(2):
                sp.wait_ge(s_out[par], 16 * (NT // 2))

        @block_.gpsimd
        def _(gp):
            nc.gpsimd.memset(ident[:, :], 0.0).then_inc(s_id0, 1)
            nc.gpsimd.memset(ones[:, :], 1.0).then_inc(s_const, 1)
            gp.wait_ge(s_id0, 1)
            nc.gpsimd.affine_select(out=ident[:, :], in_=ident[:, :], compare_op=ALU.not_equal, fill=1.0,
                                    base=0, pattern=[[-1, P]], channel_multiplier=1).then_inc(s_const, 1)
            gp.wait_ge(s_rows, 3)

            def block(b, par):
                if isinstance(b, int) and b >= NT:
                    return
                gp.wait_ge(s_xrow[par], 16 * (b // 2 + 1) if isinstance(b, int) else 8 * (b - par) + 16)
                nc.gpsimd.tensor_tensor(x_row[:, par, :], x_row[:, par, :], out_bias[:, :],
                                        ALU.add).then_inc(s_xb, 1)

            main_phase(gp, block)

        @block_.tensor
        def _(pe):
            pe.wait_ge(s_const, 2)
            pe.wait_ge(s_wm, 16)
            for i in range(DT):
                for j in range(DT):
                    last = nc.tensor.transpose(bank[i][:, j * P:(j + 1) * P], wm_sb[:, j, i * P:(i + 1) * P],
                                               ident[:, :])
                last.then_inc(s_wmT_ps, 1)
            pe.wait_ge(s_wv, 16)
            pe.wait_ge(s_wmT, DT)
            for d in range(DT):
                for i in range(DT):
                    last = nc.tensor.matmul(bank[4 + d][:, :], wv_sb[:, i, d * P:(d + 1) * P], wmT[:, i, :],
                                            start=(i == 0), stop=(i == DT - 1))
                last.then_inc(s_vproj_ps, 1)
            pe.wait_ge(s_wq, 16)
            pe.wait_ge(s_wk, 16)
            for e in range(DT):
                for j in range(DT):
                    last = nc.tensor.matmul(bank[e][:, :], wq_sb[:, j, e * P:(e + 1) * P], wk_sb[:, j, :],
                                            start=(j == 0), stop=(j == DT - 1))
                last.then_inc(s_a_ps, 1)
            pe.wait_ge(s_rep, 3)
            pe.wait_ge(s_vproj, DT)
            for j in range(DT):
                nc.tensor.matmul(bank[4][:, :], b_rep[:, 1, j, :], wq_sb[:, j, :], start=(j == 0), stop=(j == DT - 1))
            pe.wait_ge(s_bm, 16)
            for i in range(DT):
                nc.tensor.matmul(bank[5][:, :], b_rep[:, 2, i, :], wmT[:, i, :], start=(i == 0), stop=False)
            nc.tensor.matmul(bank[5][:, :], ones[0:1, :], bm_row[:, :], start=False, stop=True)
            for f in range(DT):
                for j in range(DT):
                    nc.tensor.matmul(bank[6][:, f:f + 1], wk_sb[:, j, f * P:(f + 1) * P], b_cols[:, 0, j:j + 1],
                                     start=(j == 0), stop=(j == DT - 1))
            for j in range(DT):
                nc.tensor.matmul(bank[6][:, DT:DT + 1], b_rep[:, 0, j, :], b_cols[:, 1, j:j + 1],
                                 start=(j == 0), stop=(j == DT - 1))
            for j in range(DT):
                last = nc.tensor.matmul(bank[7][:, :], b_rep[:, 0, j, :], wk_sb[:, j, :],
                                        start=(j == 0), stop=(j == DT - 1))
            last.then_inc(s_rows_ps, 1)
            pe.wait_ge(s_rows, 1)
            pe.wait_ge(s_asq, DT)
            for e in range(DT):
                last = nc.tensor.matmul(bank[4][:, :], ones[:, :], a_sq[:, e, :], start=(e == 0), stop=(e == DT - 1))
            last.then_inc(s_norm_ps, 1)

            pe.wait_ge(s_a, DT)

            def transpose_value(t, r):
                pe.wait_ge(s_val[r], 16 * (t // 4 + 1) if isinstance(t, int) else 4 * (t - r) + 16)
                if not (isinstance(t, int) and t < 2):
                    pe.wait_ge(s_valT, t - 1)
                for d in range(DT):
                    last = nc.tensor.transpose(bank[r % 2][:, d * P:(d + 1) * P],
                                               val_in[:, r, d * P:(d + 1) * P], ident[:, :])
                last.then_inc(s_vtr, 1)

            transpose_value(0, 0)

            def value_tile(t, r, last_one):
                if not last_one:
                    transpose_value(t + 1, (r + 1) % 4) if r < 3 else transpose_next(t)
                pe.wait_ge(s_valT, t + 1)
                if not (isinstance(t, int) and t < 2):
                    pe.wait_ge(s_v, t - 1)
                for d in range(DT):
                    last = nc.tensor.matmul(bank[2 + r % 2][:, :], valT[:, r % 2, d * P:(d + 1) * P],
                                            vproj[:, d, :], start=(d == 0), stop=(d == DT - 1))
                last.then_inc(s_vmm, 1)

            def transpose_next(t):
                transpose_value(t + 1, 0)

            value_phase(pe, value_tile)

            pe.wait_ge(s_kvmax, 1)
            pe.wait_ge(s_rows, 4)
            for i in range(2):
                last = nc.tensor.matmul(bank[6][0:1, i * P:(i + 1) * P], kv_max[:, i:i + 1], ident[:, :],
                                        start=True, stop=True)
            last.then_inc(s_kvT, 1)
            pe.wait_ge(s_kvrow, 1)
            nc.tensor.matmul(bank[6][:, 0:2], ones[0:1, :], kv_row[:, :], start=True, stop=True).then_inc(s_kvall, 1)
            pe.wait_ge(s_valT, NT)
            pe.wait_ge(s_v, NT)

            def prepare(s, par):
                pe.wait_ge(s_h, s + 1)
                for e in range(DT):
                    if not (isinstance(s, int) and s == 0 and e < 2):
                        pe.wait_ge(s_hT, DT * s + e - 1)
                    for r in range(CT):
                        last = nc.tensor.transpose(bank[e % 2][:, r * P:(r + 1) * P],
                                                   x_in[par][:, r, e * P:(e + 1) * P], ident[:, :])
                    last.then_inc(s_hT_ps, 1)

            def project(s, par):
                pe.wait_ge(s_hT, DT * (s + 1))
                for f in range(DT):
                    first = isinstance(s, int) and s == 0 and f < 2
                    if not first:
                        pe.wait_ge(s_q32, DT * s + f - 1)
                    for e in range(DT):
                        last = nc.tensor.matmul(bank[2 + f % 2][:, :], a_sb[:, e, f * P:(f + 1) * P],
                                                hT[par][:, e, :], start=(e == 0), stop=(e == DT - 1))
                    last.then_inc(s_q_ps, 1)
                    if not first:
                        pe.wait_ge(s_klo, DT * s + f - 1)
                    if isinstance(s, int) and s == 0:
                        pe.wait_ge(s_key[f], 16 * NS)
                    for d in range(DT):
                        src = tile_of(key_sb, s * CT + f)[:, d * P:(d + 1) * P]
                        last = nc.tensor.transpose(bank[4 + f % 2][:, d * P:(d + 1) * P], src, ident[:, :])
                    last.then_inc(s_kT_ps, 1)

            prepare(0, 0)
            prepare(1, 1)
            for s in range(NS):
                project(s, s % 2)
                if s + 2 < NS:
                    prepare(s + 2, s % 2)

            pe.wait_ge(s_klo, NT)
            pe.wait_ge(s_vlo, NT)
            pe.wait_ge(s_q32, NT)
            pe.wait_ge(s_hT, NT)

            def block(b, par):
                for c in range(NC):
                    if not (isinstance(b, int) and b >= NT):
                        if c == 0:
                            pe.wait_ge(s_qT[par], 16 * (b // 2 + 1) if isinstance(b, int) else 8 * (b - par) + 16)
                        if not (isinstance(b, int) and b == 0 and c < 4):
                            pe.wait_ge(s_score, NC * b + c - 3)
                        for i, (f, hq, hk) in enumerate([(f, *hh) for f in range(DT) for hh in ((0, 0), (0, 1), (1, 0))]):
                            last = nc.tensor.matmul(bank[c % 4][:, :], qT[:, par, f, hq, :],
                                                    k16[:, c * CT:(c + 1) * CT, hk, f, :],
                                                    start=(i == 0), stop=(i == 3 * DT - 1))
                        last.then_inc(s_qk, 1)
                    at = lagged(b, c, HLAG)
                    if at:
                        tb, tc, back = at
                        src = probs[(par + back) % 2]
                        if tc == 0:
                            pe.wait_ge(s_exp, tb + 1)
                        if not (isinstance(tb, int) and tb == 0 and tc < 2):
                            pe.wait_ge(s_plo, NC * tb + tc - 1)
                        for k in range(CT):
                            m = tc * CT + k
                            last = nc.tensor.transpose(bank[4 + tc % 2][:, k * P:(k + 1) * P],
                                                       src[:, m * P:(m + 1) * P], ident[:, :])
                        last.then_inc(s_tr, 1)
                    at = lagged(b, c, VLAG)
                    if at:
                        vb, vc, back = at
                        pe.wait_ge(s_plo, NC * vb + vc + 1)
                        if vc == 0 and not (isinstance(vb, int) and vb < 2):
                            pe.wait_ge(s_fin, vb - 1)
                        o = bank[6 + (par + back) % 2]
                        for k in range(CT):
                            m = vc * CT + k
                            for i, (hp, hv) in enumerate(((0, 0), (0, 1), (1, 0))):
                                last = nc.tensor.matmul(o[:, :], pT[:, vc % 2, hp, k * P:(k + 1) * P], v16[:, m, hv, :],
                                                        start=(m == 0 and i == 0), stop=(m == NT - 1 and i == 2))
                        last.then_inc(s_pv, 1)

            main_phase(pe, block)

        @block_.scalar
        def _(act):
            def copy_banks(first, dst, ready, done):
                for i in range(DT):
                    act.wait_ge(ready, i + 1)
                    nc.scalar.activation(dst[:, i, :], bank[first + i][:, :], ACT.Copy).then_inc(done, 1)

            copy_banks(0, wmT, s_wmT_ps, s_wmT)
            copy_banks(4, vproj, s_vproj_ps, s_vproj)
            act.wait_ge(s_vproj_ps, DT)
            copy_banks(0, a_sb, s_a_ps, s_a)
            for i in range(DT):
                act.wait_ge(s_a, i + 1)
                nc.scalar.activation(a_sq[:, i, :], a_sb[:, i, :], ACT.Square).then_inc(s_asq, 1)

            def value_tile(t, r, last_one):
                if not (isinstance(t, int) and t < 2):
                    act.wait_ge(s_vmm, t - 1)
                act.wait_ge(s_vtr, t + 1)
                nc.scalar.activation(valT[:, r % 2, :], bank[r % 2][:, :], ACT.Copy).then_inc(s_valT, 1)
                if not (isinstance(t, int) and t == 0):
                    prev = t - 1
                    act.wait_ge(s_vmm, t)
                    nc.scalar.activation(tile_of(v_sb, t), bank[2 + (r + 1) % 2][:, :], ACT.Copy).then_inc(s_v, 1)
                if last_one:
                    act.wait_ge(s_vmm, t + 1)
                    nc.scalar.activation(tile_of(v_sb, t + 1), bank[2 + r % 2][:, :], ACT.Copy).then_inc(s_v, 1)

            value_phase(act, value_tile)
            act.wait_ge(s_bound2, 1)
            nc.scalar.activation(top3[:, 2:3], q_sq[:, 0:1], ACT.Sqrt).then_inc(s_bound, 1)

            def prepare(s, par):
                act.wait_ge(s_var, s + 1)
                nc.scalar.activation(ln[:, 1, :], ln[:, 0, :], ACT.Sqrt).then_inc(s_sqrt, 1)
                act.wait_ge(s_lnc, s + 1)
                for r in range(CT):
                    last = nc.scalar.activation(x_in[par][:, r, :], x_in[par][:, r, :], ACT.Relu,
                                                scale=ln[:, 2, r:r + 1], bias=ln[:, 5, r:r + 1])
                last.then_inc(s_h, 1)
                if not (isinstance(s, int) and s < 2):
                    act.wait_ge(s_q_ps, DT * (s - 1))
                for e in range(DT):
                    act.wait_ge(s_hT_ps, DT * s + e + 1)
                    nc.scalar.activation(hT[par][:, e, :], bank[e % 2][:, :], ACT.Copy).then_inc(s_hT, 1)

            def project(s, par):
                if isinstance(s, int) and s == 0:
                    act.wait_ge(s_scales, 1)
                for f in range(DT):
                    act.wait_ge(s_q_ps, DT * s + f + 1)
                    if not (isinstance(s, int) and s == 0 and f < 2):
                        act.wait_ge(s_qlo, DT * s + f - 1)
                    nc.scalar.activation(qT_f32[:, f % 2, :], bank[2 + f % 2][:, :], ACT.Identity,
                                         scale=scale3[:, 2:3], bias=q_bias[:, f:f + 1]).then_inc(s_q32, 1)
                    act.wait_ge(s_kT_ps, DT * s + f + 1)
                    nc.scalar.activation(half_of(key_sb, CT * s + f, 0), bank[4 + f % 2][:, :], ACT.Copy,
                                         scale=scale3[:, 0:1]).then_inc(s_khi, 1)
                    if not (isinstance(s, int) and s == 0 and f == 0):
                        act.wait_ge(s_vlo, DT * s + f)
                    nc.scalar.activation(half_of(v_sb, CT * s + f, 0), tile_of(v_sb, CT * s + f + 1), ACT.Copy,
                                         scale=scale3[:, 1:2]).then_inc(s_vhi, 1)

            q_phase(act, prepare, project)
            act.wait_ge(s_q_ps, NT)

            def block(b, par):
                for c in range(NC):
                    if not (isinstance(b, int) and b >= NT):
                        act.wait_ge(s_qk, NC * b + c + 1)
                        if c == 0:
                            act.wait_ge(s_ccur, b + 1)
                        if not (isinstance(b, int) and b < 2):
                            act.wait_ge(s_tr, NC * b + c - 2 * NC + 1)
                        nc.scalar.activation(probs[par][:, c * 512:(c + 1) * 512], bank[c % 4][:, :], ACT.Identity,
                                             scale=inv_qk[:, 0:1], bias=c_cur[:, par:par + 1]).then_inc(s_score, 1)
                    if c == 0 and not (isinstance(b, int) and not 0 < b <= NT):
                        act.wait_ge(s_nmax, b)
                        if not (isinstance(b, int) and b < 3):
                            act.wait_ge(s_rd, b - 2)
                        nc.scalar.activation(probs[1 - par], probs[1 - par], ACT.Exp,
                                             bias=neg_max[:, 1 - par:2 - par], scale=1.0,
                                             accum_out=den[:, 1 - par:2 - par]).then_inc(s_exp, 1)
                    at = lagged(b, c, HLAG)
                    if at:
                        tb, tc, back = at
                        act.wait_ge(s_tr, NC * tb + tc + 1)
                        if not (isinstance(tb, int) and tb == 0 and tc < 2):
                            act.wait_ge(s_pv, NC * tb + tc - 1)
                        nc.scalar.activation(pT[:, tc % 2, 0, :], bank[4 + tc % 2][:, :], ACT.Copy,
                                             scale=PSCALE).then_inc(s_phi, 1)
                    if not (isinstance(b, int) and b >= NT):
                        act.wait_ge(s_times, NC * b + c + 1)
                        nc.scalar.activation(adj_half[c // 4][:, (c % 4) * 512:(c % 4 + 1) * 512],
                                             probs[par][:, c * 512:(c + 1) * 512], ACT.Abs).then_inc(s_abs, 1)

            main_phase(act, block)

        @block_.vector
        def _(dve):
            chain = [0]

            def link(ins):
                chain[0] += 1
                ins.then_inc(s_dve, 1)
                dve.wait_ge(s_dve, chain[0])

            dve.wait_ge(s_const, 2)
            dve.wait_ge(s_b, 48)
            for i in range(3):
                for j in range(DT):
                    last = nc.vector.tensor_scalar(b_rep[:, i, j, :], ones[:, :], b_cols[:, i, j:j + 1], None, ALU.mult)
                last.then_inc(s_rep, 1)
            dve.wait_ge(s_rows_ps, 1)
            nc.vector.tensor_copy(wq_bk[:, :], bank[4][:, :]).then_inc(s_rows, 1)
            nc.vector.tensor_copy(q_bias[:, :], bank[6][:, 0:DT]).then_inc(s_rows, 1)
            nc.vector.tensor_copy(out_bias[:, :], bank[5][:, :]).then_inc(s_rows, 1)
            nc.vector.tensor_copy(bq_bk[:, :], bank[6][:, DT:DT + 1]).then_inc(s_rows, 1)
            link(nc.vector.tensor_reduce(q_sq[:, 0:1], bank[7][:, :], axis=AX.X, op=ALU.max, apply_absolute_value=True))
            dve.wait_ge(s_norm_ps, 1)
            link(nc.vector.tensor_reduce(q_sq[:, 1:2], bank[4][:, :], axis=AX.X, op=ALU.max))
            link(nc.vector.tensor_tensor(q_sq[:, 2:3], q_sq[:, 0:1], q_sq[:, 0:1], ALU.mult))
            link(nc.vector.scalar_tensor_tensor(q_sq[:, 3:4], q_sq[:, 1:2], float(D), q_sq[:, 2:3], ALU.mult, ALU.add))
            nc.vector.tensor_scalar(q_sq[:, 0:1], q_sq[:, 3:4], 2.0, 1e-30, ALU.mult, ALU.max).then_inc(s_bound2, 1)

            def value_tile(t, r, last_one):
                dve.wait_ge(s_key[r], 16 * (t // 4 + 1) if isinstance(t, int) else 4 * (t - r) + 16)
                nc.vector.tensor_reduce(col(kmax, t), tile_of(key_sb, t), axis=AX.X, op=ALU.max,
                                        apply_absolute_value=True).then_inc(s_kread, 1)
                dve.wait_ge(s_v, t + 1)
                nc.vector.tensor_reduce(col(vmax, t), tile_of(v_sb, t + 1), axis=AX.X, op=ALU.max,
                                        apply_absolute_value=True).then_inc(s_vmax, 1)

            value_phase(dve, value_tile)
            dve.wait_ge(s_kread, NT)
            dve.wait_ge(s_vmax, NT)
            link(nc.vector.tensor_reduce(kv_max[:, 0:1], kmax[:, :], axis=AX.X, op=ALU.max))
            nc.vector.tensor_reduce(kv_max[:, 1:2], vmax[:, :], axis=AX.X, op=ALU.max).then_inc(s_kvmax, 1)
            dve.wait_ge(s_kvT, 1)
            nc.vector.tensor_reduce(kv_row[:, :], bank[6][0:1, 0:2 * P].rearrange("o (i p) -> o i p", i=2),
                                    axis=AX.X, op=ALU.max).then_inc(s_kvrow, 1)
            dve.wait_ge(s_kvall, 1)
            link(nc.vector.tensor_copy(top3[:, 0:2], bank[6][:, 0:2]))
            def prepare(s, par):
                dve.wait_ge(s_x[par], 16 * (s // 2 + 1) if isinstance(s, int) else 8 * (s - par) + 16)
                for r in range(CT):
                    last = nc.vector.bn_stats(stats[:, r, :], x_in[par][:, r, :])
                last.then_inc(s_ln[0], 1)
                dve.wait_ge(s_ln[0], s + 1)
                dve.nop(nofuse=True)
                for r in range(CT):
                    last = nc.vector.bn_aggr(meanvar[:, r, :], stats[:, r, :])
                last.then_inc(s_ln[1], 1)
                dve.wait_ge(s_ln[1], s + 1)
                nc.vector.tensor_scalar(ln[:, 0, :], meanvar[:, :, 1], EPS, None, ALU.add).then_inc(s_var, 1)
                dve.wait_ge(s_var, s + 1)
                dve.wait_ge(s_sqrt, s + 1)
                steps = [
                    lambda: nc.vector.reciprocal(ln[:, 2, :], ln[:, 1, :]),
                    lambda: nc.vector.tensor_tensor(ln[:, 3, :], ln[:, 2, :], ln[:, 2, :], ALU.mult),
                    lambda: nc.vector.tensor_tensor(ln[:, 4, :], ln[:, 3, :], ln[:, 0, :], ALU.mult),
                    lambda: nc.vector.tensor_scalar(ln[:, 3, :], ln[:, 4, :], -0.5, 1.5, ALU.mult, ALU.add),
                    lambda: nc.vector.tensor_tensor(ln[:, 2, :], ln[:, 2, :], ln[:, 3, :], ALU.mult),
                ]
                for i, step in enumerate(steps):
                    step().then_inc(s_ln[2 + i], 1)
                    dve.wait_ge(s_ln[2 + i], s + 1)
                nc.vector.scalar_tensor_tensor(ln[:, 5, :], meanvar[:, :, 0], -1.0, ln[:, 2, :],
                                               ALU.mult, ALU.mult).then_inc(s_lnc, 1)
                dve.wait_ge(s_h, s + 1)
                for r in range(CT):
                    last = nc.vector.tensor_tensor_reduce(out=scrap[:, :], in0=x_in[par][:, r, :], in1=wq_bk[:, :],
                                                          scale=1.0, scalar=0.0, op0=ALU.mult, op1=ALU.add,
                                                          accum_out=c_raw[:, r:r + 1])
                    last.then_inc(s_scrap, 1)
                    dve.wait_ge(s_scrap, CT * s + r + 1)
                nc.vector.tensor_scalar(col(c_all, CT * s, CT), c_raw[:, :], bq_bk[:, 0:1], INV_ROOT,
                                        ALU.add, ALU.mult).then_inc(s_c, 1)

            def project(s, par):
                if isinstance(s, int) and s == 0:
                    scales()
                for f in range(DT):
                    dve.wait_ge(s_q32, DT * s + f + 1)
                    if f == 0 and not (isinstance(s, int) and s == 0):
                        dve.wait_ge(s_qout, 16 * s)
                    wide = qT_f32[:, f % 2, :].rearrange("p (r n) -> p r n", r=CT)
                    nc.vector.tensor_copy(q_stage[:, :, f, 0, :], wide).then_inc(s_qhi, 1)
                    dve.wait_ge(s_khi, DT * s + f + 1)
                    nc.vector.scalar_tensor_tensor(half_of(key_sb, CT * s + f, 1), bank[4 + f % 2][:, :],
                                                   scale3[:, 0:1], half_of(key_sb, CT * s + f, 0),
                                                   ALU.mult, ALU.subtract).then_inc(s_klo, 1)
                    dve.wait_ge(s_qhi, DT * s + f + 1)
                    nc.vector.tensor_tensor(q_stage[:, :, f, 1, :], wide, q_stage[:, :, f, 0, :],
                                            ALU.subtract).then_inc(s_qlo, 1)
                    dve.wait_ge(s_vhi, DT * s + f + 1)
                    nc.vector.scalar_tensor_tensor(half_of(v_sb, CT * s + f, 1), tile_of(v_sb, CT * s + f + 1),
                                                   scale3[:, 1:2], half_of(v_sb, CT * s + f, 0),
                                                   ALU.mult, ALU.subtract).then_inc(s_vlo, 1)

            def scales():
                dve.wait_ge(s_bound, 1)
                link(nc.vector.tensor_scalar(top3[:, :], top3[:, :], 2.0 ** -50, None, ALU.max))
                link(nc.vector.tensor_scalar(pow3[:, :].bitcast(i32), top3[:, :].bitcast(i32), 0x7F800000, None,
                                             ALU.bitwise_and))
                link(nc.vector.reciprocal(rec3[:, :], pow3[:, :]))
                link(nc.vector.tensor_scalar(scale3[:, :], rec3[:, :], TOP, None, ALU.mult))
                link(nc.vector.tensor_scalar(inv3[:, :], pow3[:, :], 1.0 / TOP, None, ALU.mult))
                link(nc.vector.tensor_tensor(inv_qk0[:, :], inv3[:, 0:1], inv3[:, 2:3], ALU.mult))
                link(nc.vector.tensor_scalar(inv_qk[:, :], inv_qk0[:, :], INV_ROOT, None, ALU.mult))
                link(nc.vector.tensor_scalar(inv_pv[:, :], inv3[:, 1:2], 1.0 / PSCALE, None, ALU.mult))
                nc.vector.tensor_scalar(q_bias[:, :], q_bias[:, :], scale3[:, 2:3], None,
                                        ALU.mult).then_inc(s_scales, 1)

            q_phase(dve, prepare, project)
            dve.wait_ge(s_c, NS)

            def block(b, par):
                inside = not (isinstance(b, int) and b >= NT)
                if inside:
                    if not (isinstance(b, int) and b < 2):
                        dve.wait_ge(s_score, NC * (b - 1))
                    nc.vector.tensor_copy(c_cur[:, par:par + 1], col(c_all, b)).then_inc(s_ccur, 1)
                for c in range(NC):
                    chunk = probs[par][:, c * 512:(c + 1) * 512]
                    small = adj_half[c // 4][:, (c % 4) * 512:(c % 4 + 1) * 512]
                    if inside:
                        if c % 4 == 0:
                            dve.wait_ge(s_adj[c // 4], 16 * (b + 1))
                        dve.wait_ge(s_score, NC * b + c + 1)
                        nc.vector.tensor_tensor(chunk, chunk, small, ALU.mult).then_inc(s_times, 1)
                    at = lagged(b, c, HLAG)
                    if at:
                        tb, tc, back = at
                        dve.wait_ge(s_phi, NC * tb + tc + 1)
                        nc.vector.scalar_tensor_tensor(pT[:, tc % 2, 1, :], bank[4 + tc % 2][:, :], PSCALE,
                                                       pT[:, tc % 2, 0, :], ALU.mult, ALU.subtract).then_inc(s_plo, 1)
                    if inside:
                        dve.wait_ge(s_abs, NC * b + c + 1)
                        nc.vector.tensor_scalar(small, small, LIMIT, MASKED, ALU.is_lt, ALU.mult).then_inc(s_mask, 1)
                        dve.wait_ge(s_mask, NC * b + c + 1)
                        dve.nop(nofuse=True)
                        nc.vector.tensor_tensor_reduce(out=chunk, in0=chunk, in1=small, scale=1.0, scalar=-3.0e38,
                                                       op0=ALU.add, op1=ALU.max,
                                                       accum_out=chunk_max[:, c:c + 1]).then_inc(s_masked, 1)
                    if c == (VLAG + NC - 1) % NC + 1:
                        ob = b - 2
                        if not isinstance(b, int) or 0 <= ob < NT:
                            finish(ob, par)
                if inside:
                    dve.wait_ge(s_masked, NC * (b + 1))
                    nc.vector.tensor_reduce(neg_max[:, par:par + 1], chunk_max[:, :], axis=AX.X, op=ALU.max,
                                            negate=True).then_inc(s_nmax, 1)

            def finish(b, par):
                dve.wait_ge(s_exp, b + 1)
                nc.vector.reciprocal(rden[:, par:par + 1], den[:, par:par + 1]).then_inc(s_rd, 1)
                dve.wait_ge(s_rd, b + 1)
                nc.vector.tensor_scalar(rden[:, par:par + 1], rden[:, par:par + 1], inv_pv[:, 0:1], None,
                                        ALU.mult).then_inc(s_rden, 1)
                dve.wait_ge(s_rden, b + 1)
                dve.wait_ge(s_pv, NC * (b + 1))
                dve.wait_ge(s_xb, b + 1)
                if not (isinstance(b, int) and b < 2):
                    dve.wait_ge(s_out[par], 8 * (b - par))
                nc.vector.scalar_tensor_tensor(o_row[:, par, :], bank[6 + par][:, :], rden[:, par:par + 1],
                                               x_row[:, par, :], ALU.mult, ALU.add).then_inc(s_fin, 1)

            main_phase(dve, block)


_INS = ['x', 'adj', 'L0_gnn_key', 'L0_gnn_value', 'L0_gnn_Wq', 'L0_gnn_bq', 'L0_gnn_Wk', 'L0_gnn_bk',
        'L0_gnn_Wv', 'L0_gnn_bv', 'L0_gnn_Wm', 'L0_gnn_bm']
_OUTS = [((4096, 512), 'float32')]


def kernel(**inputs):
    import numpy as _np
    import concourse.bacc as _bacc
    from concourse import mybir as _mybir
    from concourse.bass_utils import run_bass_kernel_spmd as _run

    nc = _bacc.Bacc("TRN2", target_bir_lowering=False, num_devices=1)
    arrays, args = {}, []
    for name in _INS:
        a = _np.ascontiguousarray(inputs[name])
        arrays[f"in_{name}_dram"] = a
        args.append(nc.dram_tensor(f"in_{name}_dram", a.shape, _mybir.dt.from_np(a.dtype), kind="ExternalInput").ap())
    for i, (shape, dtype) in enumerate(_OUTS):
        dt = _mybir.dt.from_np(_np.dtype(dtype))
        args.append(nc.dram_tensor(f"out_{i}_dram", shape, dt, kind="ExternalOutput").ap())
    adjacency_attention(nc, *args)
    r = _run(nc, [arrays], core_ids=[0])
    got = tuple(r.results[0][f"out_{i}_dram"] for i in range(len(_OUTS)))
    return got[0]
```

```python
import concourse.bass as bass
from concourse import mybir
from contextlib import ExitStack


def adjacency_attention(
    nc: bass.Bass,
    x: bass.AP,
    adj: bass.AP,
    key: bass.AP,
    value: bass.AP,
    Wq: bass.AP,
    bq: bass.AP,
    Wk: bass.AP,
    bk: bass.AP,
    Wv: bass.AP,
    bv: bass.AP,
    Wm: bass.AP,
    bm: bass.AP,
    out: bass.AP,
):
    fp32 = mybir.dt.float32
    fp16 = mybir.dt.float16
    i32 = mybir.dt.int32
    ALU = mybir.AluOpType
    ACT = mybir.ActivationFunctionType
    AX = mybir.AxisListType

    N, D = x.shape
    P = 128
    NT = N // P
    DT = D // P
    NC = N // 512
    CT = 512 // P
    NS = NT // CT
    EPS = 1e-5
    LIMIT = 1e-5
    MASKED = -1e9
    INV_ROOT = 1.0 / float(N) ** 0.5
    TOP = 2.0 ** 14
    PSCALE = 2.0 ** 14
    PAIRS = NC // 2
    VLAG = NC + 3

    q_scratch = nc.dram_tensor("q_scratch", [NT, P, DT, 2, P], fp16, kind="Internal").ap()

    ctx = ExitStack()
    with ctx:
        def sb(name, shape, dt=fp32):
            return ctx.enter_context(nc.sbuf_tensor(name, shape, dt))

        def sem(name):
            return ctx.enter_context(nc.semaphore(name))

        key_sb = sb("key_sb", [P, NT, D])
        v_sb = sb("v_sb", [P, NT + 1, D])
        k16 = key_sb[:, :, :].bitcast(fp16).rearrange("p t (h f m) -> p t h f m", h=2, f=DT)
        v16 = v_sb[:, :, :].bitcast(fp16).rearrange("p t (h d) -> p t h d", h=2)
        arena = sb("arena", [P, 72 * 256])
        ident = sb("ident", [P, P])
        ones = sb("ones", [P, P])
        out_bias = sb("out_bias", [P, D])
        b_cols = sb("b_cols", [P, 3, DT])
        q_bias = sb("q_bias", [P, DT])
        c_all = sb("c_all", [P, NT])
        c_cur = sb("c_cur", [P, 2])
        bq_bk = sb("bq_bk", [P, 1])
        kmax = sb("kmax", [P, NT])
        vmax = sb("vmax", [P, NT])
        kv_max = sb("kv_max", [P, 2])
        kv_row = sb("kv_row", [1, 2])
        top3 = sb("top3", [P, 3])
        pow3 = sb("pow3", [P, 3])
        rec3 = sb("rec3", [P, 3])
        scale3 = sb("scale3", [P, 3])
        inv3 = sb("inv3", [P, 3])
        q_sq = sb("q_sq", [P, 2 * DT])
        bound_sq = sb("bound_sq", [P, 3])
        inv_qk = sb("inv_qk", [P, 1])
        inv_qk0 = sb("inv_qk0", [P, 1])
        inv_pv = sb("inv_pv", [P, 1])
        stats = sb("stats", [P, NT, 6])
        ln_v = sb("ln_v", [P, NT])
        ln_t = sb("ln_t", [P, 3, NT])
        ln_root = sb("ln_root", [P, NT])
        ln_scale = sb("ln_scale", [P, NT])
        ln_bias = sb("ln_bias", [P, NT])
        c_raw = sb("c_raw", [P, 2, CT])
        chunk_max = sb("chunk_max", [P, NC])
        neg_max = sb("neg_max", [P, 2])
        den = sb("den", [P, 2])
        rden = sb("rden", [P, 2])

        def kib(at, size, shape=None, **dims):
            view = arena[:, at * 256:(at + size) * 256]
            return view.rearrange(shape, **dims) if shape else view

        wq_sb = kib(0, 8, "p (t n) -> p t n", t=DT)
        wk_sb = kib(8, 8, "p (t n) -> p t n", t=DT)
        wv_sb = kib(16, 8, "p (t n) -> p t n", t=DT)
        wm_sb = kib(24, 8, "p (t n) -> p t n", t=DT)
        wmT = kib(40, 8, "p (t n) -> p t n", t=DT)
        vproj = kib(32, 8, "p (t n) -> p t n", t=DT)
        a_sb = kib(16, 8, "p (t n) -> p t n", t=DT)
        b_rep = kib(48, 6, "p (b t n) -> p b t n", b=3, t=DT)
        a_sq = kib(56, 2)
        bm_row = kib(58, 2)[0:1, :]
        scrap = kib(64, 2)
        wq_bk = kib(66, 2)
        x_stat = kib(68, 4, "p (s n) -> p s n", s=2)
        val_in = kib(24, 8, "p (s n) -> p s n", s=4)
        valT = kib(40, 4, "p (s n) -> p s n", s=2)
        x_in = [kib(24, 8, "p (r n) -> p r n", r=CT), kib(56, 8, "p (r n) -> p r n", r=CT)]
        hT = [kib(0, 8, "p (f n) -> p f n", f=DT), kib(8, 8, "p (f n) -> p f n", f=DT)]
        qT_f32 = kib(44, 4, "p (s n) -> p s n", s=2)
        q_stage = kib(48, 8).bitcast(fp16).rearrange("p (r f h n) -> p r f h n", r=CT, f=DT, h=2)
        probs = [kib(0, 16), kib(16, 16)]
        adj_half = [kib(32, 8), kib(40, 8)]
        p_pair = [kib(48 + 4 * i, 4).bitcast(fp16) for i in range(2)]
        pT = [kib(56 + 4 * i, 4).bitcast(fp16).rearrange("p (h k n) -> p h k n", h=2, n=P) for i in range(2)]
        qT = kib(64, 4).bitcast(fp16).rearrange("p (s f h n) -> p s f h n", s=2, f=DT, h=2)
        x_row = kib(68, 4, "p (s n) -> p s n", s=2)
        bank = [ctx.enter_context(nc.psum_tensor(f"bank{i}", [P, 512], fp32)) for i in range(8)]

        s_wm, s_wv, s_wq, s_wk, s_b = (sem(n) for n in ("s_wm", "s_wv", "s_wq", "s_wk", "s_b"))
        s_bm = sem("s_bm")
        s_id0 = sem("s_id0")
        s_const = sem("s_const")
        s_rep = sem("s_rep")
        s_wmT_ps = sem("s_wmT_ps")
        s_wmT = sem("s_wmT")
        s_vproj_ps = sem("s_vproj_ps")
        s_vproj = sem("s_vproj")
        s_a_ps = sem("s_a_ps")
        s_a = sem("s_a")
        s_asq = sem("s_asq")
        s_rows_ps = sem("s_rows_ps")
        s_rows = sem("s_rows")
        s_norm_ps = sem("s_norm_ps")
        s_bound2 = sem("s_bound2")
        s_bound = sem("s_bound")
        s_val = [sem(f"s_val{i}") for i in range(4)]
        s_key = [sem(f"s_key{i}") for i in range(4)]
        s_vtr = sem("s_vtr")
        s_valT = sem("s_valT")
        s_vmm = sem("s_vmm")
        s_v = sem("s_v")
        s_kread = sem("s_kread")
        s_vmax = sem("s_vmax")
        s_kvmax = sem("s_kvmax")
        s_kvT = sem("s_kvT")
        s_kvrow = sem("s_kvrow")
        s_kvall = sem("s_kvall")
        s_scales = sem("s_scales")
        s_dve = sem("s_dve")
        s_x = [sem(f"s_x{i}") for i in range(2)]
        s_xs = [sem(f"s_xs{i}") for i in range(2)]
        s_stat = sem("s_stat")
        s_var = sem("s_var")
        s_sqrt = sem("s_sqrt")
        s_ln = sem("s_ln")
        s_scrap = sem("s_scrap")
        s_h = sem("s_h")
        s_c = sem("s_c")
        s_hT_ps = sem("s_hT_ps")
        s_hT = sem("s_hT")
        s_q_ps = sem("s_q_ps")
        s_q32 = sem("s_q32")
        s_qhi = sem("s_qhi")
        s_qlo = sem("s_qlo")
        s_qout = sem("s_qout")
        s_kT_ps = sem("s_kT_ps")
        s_khi = sem("s_khi")
        s_klo = sem("s_klo")
        s_vhi = sem("s_vhi")
        s_vlo = sem("s_vlo")
        s_adj = [sem(f"s_adj{i}") for i in range(2)]
        s_qT = [sem(f"s_qT{i}") for i in range(2)]
        s_xrow = [sem(f"s_xrow{i}") for i in range(2)]
        s_xb = sem("s_xb")
        s_ccur = sem("s_ccur")
        s_qk = sem("s_qk")
        s_score = sem("s_score")
        s_times = sem("s_times")
        s_abs = sem("s_abs")
        s_mask = sem("s_mask")
        s_masked = sem("s_masked")
        s_nmax = sem("s_nmax")
        s_exp = sem("s_exp")
        s_phi = sem("s_phi")
        s_plo = sem("s_plo")
        s_pT = [sem(f"s_pT{i}") for i in range(2)]
        s_pv = sem("s_pv")
        s_rd = sem("s_rd")
        s_rden = sem("s_rden")
        s_fin = sem("s_fin")
        s_out = [sem(f"s_out{i}") for i in range(2)]

        x_t = x.rearrange("(t p) d -> t p d", p=P)
        x_s = x.rearrange("(s r p) d -> s p r d", p=P, r=CT)
        key_t = key.rearrange("(t p) d -> t p d", p=P)
        val_t = value.rearrange("(t p) d -> t p d", p=P)
        adj_t = adj.rearrange("(t p) (h m) -> t h p m", p=P, h=2)
        out_t = out.rearrange("(t p) d -> t p d", p=P)

        def row(view, b):
            if isinstance(b, int):
                return view[b]
            rest = " ".join("bcdef"[:len(view.shape) - 2])
            return view[bass.ds(b, 1)].rearrange(f"o a {rest} -> (o a) {rest}")

        def col(view, b, n=1):
            return view[:, b:b + n] if isinstance(b, int) else view[:, bass.ds(b, n)]

        def tile_of(tensor, t):
            if isinstance(t, int):
                return tensor[:, t, :]
            return tensor[:, bass.ds(t, 1), :].rearrange("p o n -> p (o n)")

        def half_of(tensor, t, h):
            view = tensor[:, :, :].bitcast(fp16)
            if isinstance(t, int):
                return view[:, t, h * D:(h + 1) * D]
            return view[:, bass.ds(t, 1), h * D:(h + 1) * D].rearrange("p o n -> p (o n)")

        def value_phase(eng, tile):
            for r in range(4):
                tile(r, r, False)
            with eng.Fori(4, NT - 7, 4) as t:
                for r in range(4):
                    tile(t + r, r, False)
            for r in range(4):
                tile(NT - 4 + r, r, r == 3)

        def q_phase(eng, group):
            for s in (-2, -1, 0, 1):
                group(s, s % 2)
            with eng.Fori(2, NS - 3, 2) as s:
                group(s, 0)
                group(s + 1, 1)
            for s in (NS - 2, NS - 1):
                group(s, s % 2)

        def main_phase(eng, block):
            for b in range(4):
                block(b, b % 2)
            with eng.Fori(4, NT - 3, 2) as b:
                block(b, 0)
                block(b + 1, 1)
            for b in range(NT - 2, NT + 2):
                block(b, b % 2)

        def inside(i, count, ahead=0):
            return not isinstance(i, int) or 0 <= i + ahead < count

        def early(i, first):
            return isinstance(i, int) and i < first

        def lagged(b, c, lag):
            back = (lag - c + NC - 1) // NC if lag > c else 0
            blk, chunk = b - back, c - lag + back * NC
            if isinstance(b, int) and not 0 <= blk < NT:
                return None
            return blk, chunk, back

        block_ = ctx.enter_context(nc.Block())

        @block_.sync
        def _(sp):
            sp.dma_start(wm_sb, Wm.rearrange("(t p) n -> p t n", p=P)).then_inc(s_wm, 16)
            sp.dma_start(wv_sb, Wv.rearrange("(t p) n -> p t n", p=P)).then_inc(s_wv, 16)
            for i, b in enumerate((bq, bk)):
                sp.dma_start(b_cols[:, i, :], b.rearrange("(p t) -> p t", p=P)).then_inc(s_b, 16)
            sp.dma_start(b_cols[:, 2, :], bv.rearrange("(t p) -> p t", p=P), allow_slow_non_contiguous=True).then_inc(s_b, 16)
            sp.dma_start(bm_row, bm.rearrange("(o n) -> o n", o=1)).then_inc(s_bm, 16)
            sp.dma_start(wq_sb, Wq.rearrange("(p t) n -> p t n", p=P)).then_inc(s_wq, 16)
            sp.dma_start(wk_sb, Wk.rearrange("(p t) n -> p t n", p=P)).then_inc(s_wk, 16)
            sp.wait_ge(s_wmT_ps, DT)

            def load_tile(t, r, last):
                if not (isinstance(t, int) and t < 4):
                    sp.wait_ge(s_vtr, t - 3)
                sp.dma_start(val_in[:, r, :], row(val_t, t)).then_inc(s_val[r], 16)
                if not (isinstance(t, int) and t < 4):
                    sp.wait_ge(s_kread, t - 3)
                sp.dma_start(tile_of(key_sb, t), row(key_t, t)).then_inc(s_key[r], 16)
                if not (isinstance(t, int) and t < 2):
                    sp.wait_ge(s_stat, t - 1)
                sp.dma_start(x_stat[:, r % 2, :], row(x_t, t)).then_inc(s_xs[r % 2], 16)

            value_phase(sp, load_tile)
            sp.wait_ge(s_vtr, NT)
            sp.wait_ge(s_norm_ps, 1)

            def group(s, par):
                if inside(s, NS, 2):
                    if not early(s, 0):
                        sp.wait_ge(s_hT_ps, DT * (s + 1))
                        sp.wait_ge(s_c, s + 1)
                    sp.dma_start(x_in[par], row(x_s, s + 2)).then_inc(s_x[par], 16)
                if not early(s, 0):
                    sp.wait_ge(s_qlo, DT * (s + 1))
                    dst = q_scratch.rearrange("(s r) p f h n -> s p r (f h n)", r=CT)
                    sp.dma_start(row(dst, s), q_stage.rearrange("p r f h n -> p r (f h n)")).then_inc(s_qout, 16)

            q_phase(sp, group)
            sp.wait_ge(s_qout, 16 * NS)
            sp.wait_ge(s_stat, NT)
            sp.wait_ge(s_c, NS)

            def load_q(b, par):
                sp.dma_start(qT[:, par].rearrange("p f h n -> p (f h n)"),
                             row(q_scratch, b).rearrange("p f h n -> p (f h n)")).then_inc(s_qT[par], 16)

            def load_adj(b, h):
                sp.dma_start(adj_half[h], row(adj_t[:, h], b)).then_inc(s_adj[h], 16)

            load_q(0, 0)
            for h in range(2):
                load_adj(0, h)

            def block(b, par):
                if inside(b, NT, 1):
                    if not early(b, 1):
                        sp.wait_ge(s_qk, NC * b)
                    load_q(b + 1, 1 - par)
                transpose(b - 1, 0)
                if not early(b, 2):
                    sp.wait_ge(s_fin, b - 1)
                    sp.dma_start(row(out_t, b - 2), x_row[:, par, :]).then_inc(s_out[par], 16)
                transpose(b - 1, 1)
                if inside(b, NT, 1):
                    sp.wait_ge(s_masked, NC * b + 4)
                    load_adj(b + 1, 0)
                transpose(b - 1, 2)
                if inside(b, NT):
                    if not early(b, 2):
                        sp.wait_ge(s_out[par], 8 * (b - par))
                    sp.dma_start(x_row[:, par, :], row(x_t, b)).then_inc(s_xrow[par], 16)
                transpose(b - 1, 3)
                if inside(b, NT, 1):
                    sp.wait_ge(s_masked, NC * b + 8)
                    load_adj(b + 1, 1)

            def transpose(b, j):
                if not inside(b, NT):
                    return
                sp.wait_ge(s_plo, PAIRS * b + j + 1)
                sp.nop(nofuse=True)
                if not (early(b, 1) and j < 2):
                    sp.wait_ge(s_pv, NC * b + 2 * j - 2)
                    sp.nop(nofuse=True)
                sp.dma_start_transpose(pT[j % 2].rearrange("p h k n -> p (h k) n"), p_pair[j % 2]
                                       ).then_inc(s_pT[j % 2], 16)

            main_phase(sp, block)
            for par in range(2):
                sp.wait_ge(s_out[par], 16 * (NT // 2))

        @block_.gpsimd
        def _(gp):
            nc.gpsimd.memset(ident[:, :], 0.0).then_inc(s_id0, 1)
            nc.gpsimd.memset(ones[:, :], 1.0).then_inc(s_const, 1)
            gp.wait_ge(s_id0, 1)
            nc.gpsimd.affine_select(out=ident[:, :], in_=ident[:, :], compare_op=ALU.not_equal, fill=1.0,
                                    base=0, pattern=[[-1, P]], channel_multiplier=1).then_inc(s_const, 1)
            gp.wait_ge(s_rows, 5)

            def block(b, par):
                if isinstance(b, int) and b >= NT:
                    return
                gp.wait_ge(s_xrow[par], 16 * (b // 2 + 1) if isinstance(b, int) else 8 * (b - par) + 16)
                nc.gpsimd.tensor_tensor(x_row[:, par, :], x_row[:, par, :], out_bias[:, :],
                                        ALU.add).then_inc(s_xb, 1)

            main_phase(gp, block)

        @block_.tensor
        def _(pe):
            pe.wait_ge(s_const, 2)
            pe.wait_ge(s_wm, 16)
            for i in range(DT):
                for j in range(DT):
                    last = nc.tensor.transpose(bank[i][:, j * P:(j + 1) * P], wm_sb[:, j, i * P:(i + 1) * P],
                                               ident[:, :])
                last.then_inc(s_wmT_ps, 1)
            pe.wait_ge(s_wv, 16)
            pe.wait_ge(s_wmT, DT)
            for d in range(DT):
                for i in range(DT):
                    last = nc.tensor.matmul(bank[4 + d][:, :], wv_sb[:, i, d * P:(d + 1) * P], wmT[:, i, :],
                                            start=(i == 0), stop=(i == DT - 1))
                last.then_inc(s_vproj_ps, 1)
            pe.wait_ge(s_wq, 16)
            pe.wait_ge(s_wk, 16)
            for e in range(DT):
                for j in range(DT):
                    last = nc.tensor.matmul(bank[e][:, :], wq_sb[:, j, e * P:(e + 1) * P], wk_sb[:, j, :],
                                            start=(j == 0), stop=(j == DT - 1))
                last.then_inc(s_a_ps, 1)
            pe.wait_ge(s_rep, 3)
            pe.wait_ge(s_vproj, DT)
            for j in range(DT):
                nc.tensor.matmul(bank[4][:, :], b_rep[:, 1, j, :], wq_sb[:, j, :], start=(j == 0), stop=(j == DT - 1))
            pe.wait_ge(s_bm, 16)
            for i in range(DT):
                nc.tensor.matmul(bank[5][:, :], b_rep[:, 2, i, :], wmT[:, i, :], start=(i == 0), stop=False)
            nc.tensor.matmul(bank[5][:, :], ones[0:1, :], bm_row, start=False, stop=True)
            for f in range(DT):
                for j in range(DT):
                    nc.tensor.matmul(bank[6][:, f:f + 1], wk_sb[:, j, f * P:(f + 1) * P], b_cols[:, 0, j:j + 1],
                                     start=(j == 0), stop=(j == DT - 1))
            for j in range(DT):
                last = nc.tensor.matmul(bank[6][:, DT:DT + 1], b_rep[:, 0, j, :], b_cols[:, 1, j:j + 1],
                                        start=(j == 0), stop=(j == DT - 1))
            last.then_inc(s_rows_ps, 1)
            pe.wait_ge(s_rows, 5)
            pe.wait_ge(s_asq, DT)
            nc.tensor.matmul(bank[7][:, 0:2 * DT], ones[:, :], q_sq[:, :], start=True, stop=True).then_inc(s_norm_ps, 1)

            pe.wait_ge(s_a, DT)

            def transpose_value(t, r):
                pe.wait_ge(s_val[r], 16 * (t // 4 + 1) if isinstance(t, int) else 4 * (t - r) + 16)
                if not (isinstance(t, int) and t < 2):
                    pe.wait_ge(s_valT, t - 1)
                for d in range(DT):
                    last = nc.tensor.transpose(bank[r % 2][:, d * P:(d + 1) * P],
                                               val_in[:, r, d * P:(d + 1) * P], ident[:, :])
                last.then_inc(s_vtr, 1)

            transpose_value(0, 0)

            def value_tile(t, r, last_one):
                if not last_one:
                    transpose_value(t + 1, (r + 1) % 4) if r < 3 else transpose_next(t)
                pe.wait_ge(s_valT, t + 1)
                if not (isinstance(t, int) and t < 2):
                    pe.wait_ge(s_v, t - 1)
                for d in range(DT):
                    last = nc.tensor.matmul(bank[2 + r % 2][:, :], valT[:, r % 2, d * P:(d + 1) * P],
                                            vproj[:, d, :], start=(d == 0), stop=(d == DT - 1))
                last.then_inc(s_vmm, 1)

            def transpose_next(t):
                transpose_value(t + 1, 0)

            value_phase(pe, value_tile)

            pe.wait_ge(s_kvmax, 1)
            pe.wait_ge(s_rows, 5)
            for i in range(2):
                last = nc.tensor.matmul(bank[6][0:1, i * P:(i + 1) * P], kv_max[:, i:i + 1], ident[:, :],
                                        start=True, stop=True)
            last.then_inc(s_kvT, 1)
            pe.wait_ge(s_kvrow, 1)
            nc.tensor.matmul(bank[6][:, 0:2], ones[0:1, :], kv_row[:, :], start=True, stop=True).then_inc(s_kvall, 1)
            pe.wait_ge(s_valT, NT)
            pe.wait_ge(s_v, NT)

            for s in range(-1, NS):
                for f in range(DT):
                    if s + 1 < NS:
                        pe.wait_ge(s_h, CT * (s + 2))
                        if DT * (s + 1) + f >= 2:
                            pe.wait_ge(s_hT, DT * (s + 1) + f - 1)
                        for r in range(CT):
                            last = nc.tensor.transpose(bank[f % 2][:, r * P:(r + 1) * P],
                                                       x_in[(s + 1) % 2][:, r, f * P:(f + 1) * P], ident[:, :])
                        last.then_inc(s_hT_ps, 1)
                    if s < 0:
                        continue
                    pe.wait_ge(s_hT, DT * (s + 1))
                    if DT * s + f >= 2:
                        pe.wait_ge(s_q32, DT * s + f - 1)
                    for e in range(DT):
                        last = nc.tensor.matmul(bank[2 + f % 2][:, :], a_sb[:, e, f * P:(f + 1) * P],
                                                hT[s % 2][:, e, :], start=(e == 0), stop=(e == DT - 1))
                    last.then_inc(s_q_ps, 1)
                    if DT * s + f >= 2:
                        pe.wait_ge(s_klo, DT * s + f - 1)
                    if s == 0:
                        pe.wait_ge(s_key[f], 16 * NS)
                    for d in range(DT):
                        last = nc.tensor.transpose(bank[4 + f % 2][:, d * P:(d + 1) * P],
                                                   key_sb[:, s * CT + f, d * P:(d + 1) * P], ident[:, :])
                    last.then_inc(s_kT_ps, 1)

            pe.wait_ge(s_klo, NT)
            pe.wait_ge(s_q32, NT)
            pe.wait_ge(s_hT, NT)

            def block(b, par):
                for c in range(NC):
                    if not (isinstance(b, int) and b >= NT):
                        if c == 0:
                            pe.wait_ge(s_qT[par], 16 * (b // 2 + 1) if isinstance(b, int) else 8 * (b - par) + 16)
                        if not (isinstance(b, int) and b == 0 and c < 4):
                            pe.wait_ge(s_score, NC * b + c - 3)
                        for i, (f, hq, hk) in enumerate([(f, *hh) for f in range(DT) for hh in ((0, 0), (0, 1), (1, 0))]):
                            last = nc.tensor.matmul(bank[c % 4][:, :], qT[:, par, f, hq, :],
                                                    k16[:, c * CT:(c + 1) * CT, hk, f, :],
                                                    start=(i == 0), stop=(i == 3 * DT - 1))
                        last.then_inc(s_qk, 1)
                    at = lagged(b, c, VLAG)
                    if at:
                        vb, vc, back = at
                        j = vc // 2
                        if vc % 2 == 0:
                            pe.wait_ge(s_pT[j % 2], 16 * (2 * vb + j // 2 + 1))
                        if isinstance(vb, int) and vb == 0:
                            pe.wait_ge(s_vlo, CT * (vc + 1))
                        if vc == 0 and not (isinstance(vb, int) and vb < 2):
                            pe.wait_ge(s_fin, vb - 1)
                        o = bank[6 + (par + back) % 2]
                        for k in range(CT):
                            m = vc * CT + k
                            for i, (hp, hv) in enumerate(((0, 0), (0, 1), (1, 0))):
                                last = nc.tensor.matmul(o[:, :], pT[j % 2][:, hp, vc % 2 * CT + k, :], v16[:, m, hv, :],
                                                        start=(m == 0 and i == 0), stop=(m == NT - 1 and i == 2))
                        last.then_inc(s_pv, 1)

            main_phase(pe, block)

        @block_.scalar
        def _(act):
            def copy_banks(first, dst, ready, done):
                for i in range(DT):
                    act.wait_ge(ready, i + 1)
                    nc.scalar.activation(dst[:, i, :], bank[first + i][:, :], ACT.Copy).then_inc(done, 1)

            copy_banks(0, wmT, s_wmT_ps, s_wmT)
            copy_banks(4, vproj, s_vproj_ps, s_vproj)
            act.wait_ge(s_vproj_ps, DT)
            copy_banks(0, a_sb, s_a_ps, s_a)
            for i in range(DT):
                act.wait_ge(s_a, i + 1)
                if i:
                    act.wait_ge(s_asq, i)
                nc.scalar.activation(a_sq[:, :], a_sb[:, i, :], ACT.Square,
                                     accum_out=q_sq[:, i:i + 1]).then_inc(s_asq, 1)

            def value_tile(t, r, last_one):
                if not (isinstance(t, int) and t < 2):
                    act.wait_ge(s_vmm, t - 1)
                act.wait_ge(s_vtr, t + 1)
                nc.scalar.activation(valT[:, r % 2, :], bank[r % 2][:, :], ACT.Copy).then_inc(s_valT, 1)
                if not (isinstance(t, int) and t == 0):
                    prev = t - 1
                    act.wait_ge(s_vmm, t)
                    nc.scalar.activation(tile_of(v_sb, t), bank[2 + (r + 1) % 2][:, :], ACT.Copy).then_inc(s_v, 1)
                if last_one:
                    act.wait_ge(s_vmm, t + 1)
                    nc.scalar.activation(tile_of(v_sb, t + 1), bank[2 + r % 2][:, :], ACT.Copy).then_inc(s_v, 1)

            value_phase(act, value_tile)
            act.wait_ge(s_bound2, 1)
            nc.scalar.activation(top3[:, 2:3], bound_sq[:, 2:3], ACT.Sqrt).then_inc(s_bound, 1)
            act.wait_ge(s_var, 1)
            nc.scalar.activation(ln_root[:, :], ln_v[:, :], ACT.Sqrt).then_inc(s_sqrt, 1)

            def group(s, par):
                for f in range(DT):
                    if inside(s, NS, 1) and not early(s, -1):
                        if not early(s, 1) and f == 0:
                            act.wait_ge(s_q_ps, DT * s)
                        act.wait_ge(s_hT_ps, DT * (s + 1) + f + 1)
                        nc.scalar.activation(hT[1 - par][:, f, :], bank[f % 2][:, :], ACT.Copy).then_inc(s_hT, 1)
                    if inside(s, NS):
                        act.wait_ge(s_q_ps, DT * s + f + 1)
                        if not (early(s, 1) and f < 2):
                            act.wait_ge(s_qlo, DT * s + f - 1)
                        nc.scalar.activation(qT_f32[:, f % 2, :], bank[2 + f % 2][:, :], ACT.Identity,
                                             scale=scale3[:, 2:3], bias=q_bias[:, f:f + 1]).then_inc(s_q32, 1)
                    if inside(s, NS, 2):
                        if f == 0:
                            act.wait_ge(s_x[par], 8 * (s + 2 - par) + 16)
                        t = CT * (s + 2) + f
                        nc.scalar.activation(x_in[par][:, f, :], x_in[par][:, f, :], ACT.Relu,
                                             scale=col(ln_scale, t), bias=col(ln_bias, t)).then_inc(s_h, 1)
                    if inside(s, NS):
                        act.wait_ge(s_kT_ps, DT * s + f + 1)
                        nc.scalar.activation(half_of(key_sb, CT * s + f, 0), bank[4 + f % 2][:, :], ACT.Copy,
                                             scale=scale3[:, 0:1]).then_inc(s_khi, 1)

            act.wait_ge(s_ln, 1)
            act.wait_ge(s_scales, 1)
            q_phase(act, group)
            act.wait_ge(s_q_ps, NT)

            def block(b, par):
                for c in range(NC):
                    if not (isinstance(b, int) and b >= NT):
                        act.wait_ge(s_qk, NC * b + c + 1)
                        if c == 0:
                            act.wait_ge(s_ccur, b + 1)
                        if not early(b, 2) and c % 2 == 0:
                            act.wait_ge(s_plo, PAIRS * (b - 2) + c // 2 + 1)
                        nc.scalar.activation(probs[par][:, c * 512:(c + 1) * 512], bank[c % 4][:, :], ACT.Identity,
                                             scale=inv_qk[:, 0:1], bias=c_cur[:, par:par + 1]).then_inc(s_score, 1)
                    if c == 0 and not (isinstance(b, int) and not 0 < b <= NT):
                        act.wait_ge(s_nmax, b)
                        if not (isinstance(b, int) and b < 3):
                            act.wait_ge(s_rd, b - 2)
                        nc.scalar.activation(probs[1 - par], probs[1 - par], ACT.Exp,
                                             bias=neg_max[:, 1 - par:2 - par], scale=1.0,
                                             accum_out=den[:, 1 - par:2 - par]).then_inc(s_exp, 1)
                    if c % 2 == 1 and inside(b, NT, -1):
                        j = c // 2
                        if j == 0:
                            act.wait_ge(s_exp, b)
                        if not (early(b, 2) and j < 2):
                            act.wait_ge(s_pT[j % 2], 16 * (2 * (b - 1) + j // 2))
                        nc.scalar.activation(p_pair[j % 2][:, 0:1024], probs[1 - par][:, j * 1024:(j + 1) * 1024],
                                             ACT.Copy, scale=PSCALE).then_inc(s_phi, 1)
                    if early(b, 2):
                        for t in range(2 * (NC * b + c), 2 * (NC * b + c) + 2):
                            if t:
                                act.wait_ge(s_vlo, t)
                            nc.scalar.activation(half_of(v_sb, t, 0), tile_of(v_sb, t + 1), ACT.Copy,
                                                 scale=scale3[:, 1:2]).then_inc(s_vhi, 1)
                    if not (isinstance(b, int) and b >= NT):
                        act.wait_ge(s_times, NC * b + c + 1)
                        nc.scalar.activation(adj_half[c // 4][:, (c % 4) * 512:(c % 4 + 1) * 512],
                                             probs[par][:, c * 512:(c + 1) * 512], ACT.Abs).then_inc(s_abs, 1)

            main_phase(act, block)

        @block_.vector
        def _(dve):
            chain = [0]

            def link(ins):
                chain[0] += 1
                ins.then_inc(s_dve, 1)
                dve.wait_ge(s_dve, chain[0])

            dve.wait_ge(s_const, 2)
            dve.wait_ge(s_b, 48)
            for i in range(3):
                for j in range(DT):
                    last = nc.vector.tensor_scalar(b_rep[:, i, j, :], ones[:, :], b_cols[:, i, j:j + 1], None, ALU.mult)
                last.then_inc(s_rep, 1)
            dve.wait_ge(s_rows_ps, 1)
            nc.vector.tensor_copy(wq_bk[:, :], bank[4][:, :]).then_inc(s_rows, 1)
            nc.vector.tensor_copy(q_bias[:, :], bank[6][:, 0:DT]).then_inc(s_rows, 1)
            dve.wait_ge(s_rows, 2)
            nc.vector.tensor_tensor(q_sq[:, DT:2 * DT], q_bias[:, :], q_bias[:, :], ALU.mult).then_inc(s_rows, 1)
            nc.vector.tensor_copy(out_bias[:, :], bank[5][:, :]).then_inc(s_rows, 1)
            nc.vector.tensor_copy(bq_bk[:, :], bank[6][:, DT:DT + 1]).then_inc(s_rows, 1)
            dve.wait_ge(s_norm_ps, 1)
            link(nc.vector.tensor_reduce(bound_sq[:, 0:2], bank[7][:, 0:2 * DT].rearrange("p (i f) -> p i f", i=2),
                                         axis=AX.X, op=ALU.add))
            link(nc.vector.scalar_tensor_tensor(bound_sq[:, 2:3], bound_sq[:, 0:1], float(D), bound_sq[:, 1:2],
                                                ALU.mult, ALU.add))
            nc.vector.tensor_scalar(bound_sq[:, 2:3], bound_sq[:, 2:3], 2.0, 1e-30, ALU.mult,
                                    ALU.max).then_inc(s_bound2, 1)

            def value_tile(t, r, last_one):
                dve.wait_ge(s_key[r], 16 * (t // 4 + 1) if isinstance(t, int) else 4 * (t - r) + 16)
                nc.vector.tensor_reduce(col(kmax, t), tile_of(key_sb, t), axis=AX.X, op=ALU.max,
                                        apply_absolute_value=True).then_inc(s_kread, 1)
                dve.wait_ge(s_xs[r % 2], 16 * (t // 2 + 1) if isinstance(t, int) else 8 * (t - r % 2) + 16)
                nc.vector.bn_stats(tile_of(stats, t), x_stat[:, r % 2, :]).then_inc(s_stat, 1)
                dve.wait_ge(s_v, t + 1)
                nc.vector.tensor_reduce(col(vmax, t), tile_of(v_sb, t + 1), axis=AX.X, op=ALU.max,
                                        apply_absolute_value=True).then_inc(s_vmax, 1)

            value_phase(dve, value_tile)
            dve.wait_ge(s_kread, NT)
            dve.wait_ge(s_vmax, NT)
            link(nc.vector.tensor_reduce(kv_max[:, 0:1], kmax[:, :], axis=AX.X, op=ALU.max))
            nc.vector.tensor_reduce(kv_max[:, 1:2], vmax[:, :], axis=AX.X, op=ALU.max).then_inc(s_kvmax, 1)
            dve.wait_ge(s_kvT, 1)
            nc.vector.tensor_reduce(kv_row[:, :], bank[6][0:1, 0:2 * P].rearrange("o (i p) -> o i p", i=2),
                                    axis=AX.X, op=ALU.max).then_inc(s_kvrow, 1)
            dve.wait_ge(s_kvall, 1)
            link(nc.vector.tensor_copy(top3[:, 0:2], bank[6][:, 0:2]))
            dve.wait_ge(s_stat, NT)
            mean_e, mean_o, m2_e, m2_o = (stats[:, :, i] for i in (1, 4, 2, 5))
            link(nc.vector.tensor_tensor(ln_t[:, 0, :], mean_e, mean_o, ALU.subtract))
            link(nc.vector.tensor_tensor(ln_t[:, 1, :], m2_e, m2_o, ALU.add))
            link(nc.vector.tensor_tensor(ln_t[:, 2, :], ln_t[:, 0, :], ln_t[:, 0, :], ALU.mult))
            link(nc.vector.tensor_scalar(ln_t[:, 1, :], ln_t[:, 1, :], 1.0 / D, EPS, ALU.mult, ALU.add))
            nc.vector.scalar_tensor_tensor(ln_v[:, :], ln_t[:, 2, :], 0.25, ln_t[:, 1, :],
                                           ALU.mult, ALU.add).then_inc(s_var, 1)
            dve.wait_ge(s_bound, 1)
            link(nc.vector.tensor_scalar(top3[:, :], top3[:, :], 2.0 ** -50, None, ALU.max))
            link(nc.vector.tensor_scalar(pow3[:, :].bitcast(i32), top3[:, :].bitcast(i32), 0x7F800000, None,
                                         ALU.bitwise_and))
            link(nc.vector.reciprocal(rec3[:, :], pow3[:, :]))
            link(nc.vector.tensor_scalar(scale3[:, :], rec3[:, :], TOP, None, ALU.mult))
            link(nc.vector.tensor_scalar(inv3[:, :], pow3[:, :], 1.0 / TOP, None, ALU.mult))
            link(nc.vector.tensor_tensor(inv_qk0[:, :], inv3[:, 0:1], inv3[:, 2:3], ALU.mult))
            link(nc.vector.tensor_scalar(inv_qk[:, :], inv_qk0[:, :], INV_ROOT, None, ALU.mult))
            link(nc.vector.tensor_scalar(inv_pv[:, :], inv3[:, 1:2], 1.0 / PSCALE, None, ALU.mult))
            nc.vector.tensor_scalar(q_bias[:, :], q_bias[:, :], scale3[:, 2:3], None, ALU.mult).then_inc(s_scales, 1)
            dve.wait_ge(s_sqrt, 1)
            link(nc.vector.reciprocal(ln_scale[:, :], ln_root[:, :]))
            link(nc.vector.tensor_tensor(ln_t[:, 0, :], ln_scale[:, :], ln_scale[:, :], ALU.mult))
            link(nc.vector.tensor_tensor(ln_t[:, 1, :], ln_t[:, 0, :], ln_v[:, :], ALU.mult))
            link(nc.vector.tensor_scalar(ln_t[:, 0, :], ln_t[:, 1, :], -0.5, 1.5, ALU.mult, ALU.add))
            link(nc.vector.tensor_tensor(ln_scale[:, :], ln_scale[:, :], ln_t[:, 0, :], ALU.mult))
            link(nc.vector.tensor_tensor(ln_t[:, 2, :], mean_e, mean_o, ALU.add))
            nc.vector.scalar_tensor_tensor(ln_bias[:, :], ln_t[:, 2, :], -0.5, ln_scale[:, :],
                                           ALU.mult, ALU.mult).then_inc(s_ln, 1)

            def group(s, par):
                for f in range(DT):
                    if inside(s, NS):
                        dve.wait_ge(s_q32, DT * s + f + 1)
                        if f == 0 and not early(s, 1):
                            dve.wait_ge(s_qout, 16 * s)
                        wide = qT_f32[:, f % 2, :].rearrange("p (r n) -> p r n", r=CT)
                        nc.vector.tensor_copy(q_stage[:, :, f, 0, :], wide).then_inc(s_qhi, 1)
                    if inside(s, NS, 2):
                        dve.wait_ge(s_h, CT * (s + 2) + f + 1)
                        if not (early(s, -1) and f == 0):
                            dve.wait_ge(s_scrap, CT * (s + 2) + f)
                        nc.vector.tensor_tensor_reduce(out=scrap[:, :], in0=x_in[par][:, f, :], in1=wq_bk[:, :],
                                                       scale=1.0, scalar=0.0, op0=ALU.mult, op1=ALU.add,
                                                       accum_out=c_raw[:, par, f:f + 1]).then_inc(s_scrap, 1)
                    if inside(s, NS):
                        dve.wait_ge(s_qhi, DT * s + f + 1)
                        nc.vector.tensor_tensor(q_stage[:, :, f, 1, :], wide, q_stage[:, :, f, 0, :],
                                                ALU.subtract).then_inc(s_qlo, 1)
                        dve.wait_ge(s_khi, DT * s + f + 1)
                        nc.vector.scalar_tensor_tensor(half_of(key_sb, CT * s + f, 1), bank[4 + f % 2][:, :],
                                                       scale3[:, 0:1], half_of(key_sb, CT * s + f, 0),
                                                       ALU.mult, ALU.subtract).then_inc(s_klo, 1)
                if inside(s, NS, 2):
                    dve.wait_ge(s_scrap, CT * (s + 3))
                    nc.vector.tensor_scalar(col(c_all, CT * (s + 2), CT), c_raw[:, par, :], bq_bk[:, 0:1], INV_ROOT,
                                            ALU.add, ALU.mult).then_inc(s_c, 1)

            q_phase(dve, group)
            dve.wait_ge(s_c, NS)

            def block(b, par):
                here = inside(b, NT)
                if here:
                    if not (isinstance(b, int) and b < 2):
                        dve.wait_ge(s_score, NC * (b - 1))
                    nc.vector.tensor_copy(c_cur[:, par:par + 1], col(c_all, b)).then_inc(s_ccur, 1)
                for c in range(NC):
                    chunk = probs[par][:, c * 512:(c + 1) * 512]
                    small = adj_half[c // 4][:, (c % 4) * 512:(c % 4 + 1) * 512]
                    if here:
                        if c % 4 == 0:
                            dve.wait_ge(s_adj[c // 4], 16 * (b + 1))
                        dve.wait_ge(s_score, NC * b + c + 1)
                        nc.vector.tensor_tensor(chunk, chunk, small, ALU.mult).then_inc(s_times, 1)
                    if c % 2 == 1 and inside(b, NT, -1):
                        j = c // 2
                        dve.wait_ge(s_phi, PAIRS * (b - 1) + j + 1)
                        nc.vector.scalar_tensor_tensor(p_pair[j % 2][:, 1024:2048],
                                                       probs[1 - par][:, j * 1024:(j + 1) * 1024], PSCALE,
                                                       p_pair[j % 2][:, 0:1024],
                                                       ALU.mult, ALU.subtract).then_inc(s_plo, 1)
                    if early(b, 2):
                        for t in range(2 * (NC * b + c), 2 * (NC * b + c) + 2):
                            dve.wait_ge(s_vhi, t + 1)
                            nc.vector.scalar_tensor_tensor(half_of(v_sb, t, 1), tile_of(v_sb, t + 1), scale3[:, 1:2],
                                                           half_of(v_sb, t, 0), ALU.mult,
                                                           ALU.subtract).then_inc(s_vlo, 1)
                    if here:
                        dve.wait_ge(s_abs, NC * b + c + 1)
                        nc.vector.tensor_scalar(small, small, LIMIT, MASKED, ALU.is_lt, ALU.mult).then_inc(s_mask, 1)
                        dve.wait_ge(s_mask, NC * b + c + 1)
                        dve.nop(nofuse=True)
                        nc.vector.tensor_tensor_reduce(out=chunk, in0=chunk, in1=small, scale=1.0, scalar=-3.0e38,
                                                       op0=ALU.add, op1=ALU.max,
                                                       accum_out=chunk_max[:, c:c + 1]).then_inc(s_masked, 1)
                    if c == (VLAG + NC - 1) % NC + 1:
                        ob = b - 2
                        if not isinstance(b, int) or 0 <= ob < NT:
                            finish(ob, par)
                if here:
                    dve.wait_ge(s_masked, NC * (b + 1))
                    nc.vector.tensor_reduce(neg_max[:, par:par + 1], chunk_max[:, :], axis=AX.X, op=ALU.max,
                                            negate=True).then_inc(s_nmax, 1)

            def finish(b, par):
                dve.wait_ge(s_exp, b + 1)
                nc.vector.reciprocal(rden[:, par:par + 1], den[:, par:par + 1]).then_inc(s_rd, 1)
                dve.wait_ge(s_rd, b + 1)
                nc.vector.tensor_scalar(rden[:, par:par + 1], rden[:, par:par + 1], inv_pv[:, 0:1], None,
                                        ALU.mult).then_inc(s_rden, 1)
                dve.wait_ge(s_rden, b + 1)
                dve.wait_ge(s_pv, NC * (b + 1))
                dve.wait_ge(s_xb, b + 1)
                nc.vector.scalar_tensor_tensor(x_row[:, par, :], bank[6 + par][:, :], rden[:, par:par + 1],
                                               x_row[:, par, :], ALU.mult, ALU.add).then_inc(s_fin, 1)

            main_phase(dve, block)


_INS = ['x', 'adj', 'L0_gnn_key', 'L0_gnn_value', 'L0_gnn_Wq', 'L0_gnn_bq', 'L0_gnn_Wk', 'L0_gnn_bk',
        'L0_gnn_Wv', 'L0_gnn_bv', 'L0_gnn_Wm', 'L0_gnn_bm']
_OUTS = [((4096, 512), 'float32')]


def kernel(**inputs):
    import numpy as _np
    import concourse.bacc as _bacc
    from concourse import mybir as _mybir
    from concourse.bass_utils import run_bass_kernel_spmd as _run

    nc = _bacc.Bacc("TRN2", target_bir_lowering=False, num_devices=1)
    arrays, args = {}, []
    for name in _INS:
        a = _np.ascontiguousarray(inputs[name])
        arrays[f"in_{name}_dram"] = a
        args.append(nc.dram_tensor(f"in_{name}_dram", a.shape, _mybir.dt.from_np(a.dtype), kind="ExternalInput").ap())
    for i, (shape, dtype) in enumerate(_OUTS):
        dt = _mybir.dt.from_np(_np.dtype(dtype))
        args.append(nc.dram_tensor(f"out_{i}_dram", shape, dt, kind="ExternalOutput").ap())
    adjacency_attention(nc, *args)
    r = _run(nc, [arrays], core_ids=[0])
    got = tuple(r.results[0][f"out_{i}_dram"] for i in range(len(_OUTS)))
    return got[0]
```

```python
import concourse.bass as bass
from concourse import mybir
from contextlib import ExitStack


def adjacency_attention(
    nc: bass.Bass,
    x: bass.AP,
    adj: bass.AP,
    key: bass.AP,
    value: bass.AP,
    Wq: bass.AP,
    bq: bass.AP,
    Wk: bass.AP,
    bk: bass.AP,
    Wv: bass.AP,
    bv: bass.AP,
    Wm: bass.AP,
    bm: bass.AP,
    out: bass.AP,
):
    fp32 = mybir.dt.float32
    fp16 = mybir.dt.float16
    i32 = mybir.dt.int32
    ALU = mybir.AluOpType
    ACT = mybir.ActivationFunctionType
    AX = mybir.AxisListType

    N, D = x.shape
    P = 128
    NT = N // P
    DT = D // P
    NC = N // 512
    CT = 512 // P
    NS = NT // CT
    EPS = 1e-5
    LIMIT = 1e-5
    MASKED = -1e9
    INV_ROOT = 1.0 / float(N) ** 0.5
    TOP = 2.0 ** 14
    PSCALE = 2.0 ** 14
    HSCALE = 2.0 ** 10
    PAIRS = NC // 2
    VLAG = NC + 3

    q_scratch = nc.dram_tensor("q_scratch", [NT, P, DT, 2, P], fp16, kind="Internal").ap()

    ctx = ExitStack()
    with ctx:
        def sb(name, shape, dt=fp32):
            return ctx.enter_context(nc.sbuf_tensor(name, shape, dt))

        def sem(name):
            return ctx.enter_context(nc.semaphore(name))

        key_sb = sb("key_sb", [P, NT, D])
        v_sb = sb("v_sb", [P, NT + 1, D])
        k16 = key_sb[:, :, :].bitcast(fp16).rearrange("p t (h f m) -> p t h f m", h=2, f=DT)
        v16 = v_sb[:, :, :].bitcast(fp16).rearrange("p t (h d) -> p t h d", h=2)
        arena = sb("arena", [P, 72 * 256])
        ident = sb("ident", [P, P])
        ones = sb("ones", [P, P])
        out_bias = sb("out_bias", [P, D])
        b_cols = sb("b_cols", [P, 3, DT])
        q_bias = sb("q_bias", [P, DT])
        c_all = sb("c_all", [P, NT])
        c_cur = sb("c_cur", [P, 2])
        bq_bk = sb("bq_bk", [P, 1])
        key_sq = sb("key_sq", [P, NT])
        val_top = sb("val_top", [P, NT])
        val_steps = sb("val_steps", [P, 3, CT])
        val_scale = sb("val_scale", [P, 2, CT])
        val_undo = sb("val_undo", [P, NT])
        kv_max = sb("kv_max", [P, 2])
        kv_row = sb("kv_row", [1, 2])
        kv_all = sb("kv_all", [P, 2])
        sq_sums = sb("sq_sums", [P, 3, DT])
        fro_sq = sb("fro_sq", [P, 3])
        sc_c = sb("sc_c", [P, 5])
        sc_a = sb("sc_a", [P, 5])
        bound_sq = sb("bound_sq", [P, 3])
        sc3 = sb("sc3", [P, 5, 3])
        q_undo = sb("q_undo", [P, 2])
        inv_qk = sb("inv_qk", [P, 1])
        inv_qk0 = sb("inv_qk0", [P, 1])
        inv_pv = sb("inv_pv", [P, 1])
        ln_scale = sb("ln_scale", [P, NT])
        ln_bias = sb("ln_bias", [P, NT])
        c_raw = sb("c_raw", [P, 2, CT])
        chunk_max = sb("chunk_max", [P, NC])
        neg_max = sb("neg_max", [P, 2])
        den = sb("den", [P, 2])
        rden = sb("rden", [P, 2])

        def kib(at, size, shape=None, **dims):
            view = arena[:, at * 256:(at + size) * 256]
            return view.rearrange(shape, **dims) if shape else view

        wq_sb = v_sb[:, 17:21, :]
        wk_sb = v_sb[:, 21:25, :]
        wv_sb = kib(16, 8, "p (t n) -> p t n", t=DT)
        wm_sb = kib(24, 8, "p (t n) -> p t n", t=DT)
        wmT = kib(32, 8, "p (t n) -> p t n", t=DT)
        c_pair = kib(40, 8).bitcast(fp16).rearrange("p (d h n) -> p d h n", d=DT, h=2)
        a_pair = kib(48, 8).bitcast(fp16).rearrange("p (d h n) -> p d h n", d=DT, h=2)
        b_rep = kib(56, 6, "p (b t n) -> p b t n", b=3, t=DT)
        bm_row = kib(64, 2)[0:1, :]
        wq_bk = kib(66, 2)
        squares = kib(68, 2)
        stats = kib(70, 2)[:, 0:6 * NT].rearrange("p (t i) -> p t i", i=6)
        ln_v = kib(70, 2)[:, 6 * NT:7 * NT]
        ln_root = kib(70, 2)[:, 7 * NT:8 * NT]
        ln_t = kib(70, 2)[:, 8 * NT:11 * NT].rearrange("p (i t) -> p i t", i=3)
        x_stat = [kib(56, 4, "p (r n) -> p r n", r=2), kib(60, 4, "p (r n) -> p r n", r=2)]
        rows_in = [kib(16, 8, "p (r n) -> p r n", r=CT), kib(24, 8, "p (r n) -> p r n", r=CT)]
        row_pair = kib(32, 8).bitcast(fp16).rearrange("p (r h n) -> p r h n", r=CT, h=2)
        rowT = [kib(8 * i, 8).bitcast(fp16).rearrange("p (r h d m) -> p r h d m", r=CT, h=2, d=DT) for i in range(2)]
        key_pair = kib(40, 8).bitcast(fp16).rearrange("p (r h n) -> p r h n", r=CT, h=2)
        scrap = kib(64, 2)
        qT_f32 = kib(68, 4, "p (s n) -> p s n", s=2)
        key_buf = [key_pair] + [v.bitcast(fp16).rearrange("p r (h n) -> p r h n", h=2) for v in rows_in]
        q_stage = kib(56, 8).bitcast(fp16).rearrange("p (r f h n) -> p r f h n", r=CT, f=DT, h=2)
        probs = [kib(0, 16), kib(16, 16)]
        adj_half = [kib(32, 8), kib(40, 8)]
        p_pair = [kib(48 + 4 * i, 4).bitcast(fp16) for i in range(2)]
        pT = [kib(56 + 4 * i, 4).bitcast(fp16).rearrange("p (h k n) -> p h k n", h=2, n=P) for i in range(2)]
        qT = kib(64, 4).bitcast(fp16).rearrange("p (s f h n) -> p s f h n", s=2, f=DT, h=2)
        x_row = kib(68, 4, "p (s n) -> p s n", s=2)
        bank = [ctx.enter_context(nc.psum_tensor(f"bank{i}", [P, 512], fp32)) for i in range(8)]

        s_wm, s_wv, s_wq, s_wk, s_b = (sem(n) for n in ("s_wm", "s_wv", "s_wq", "s_wk", "s_b"))
        s_bm = sem("s_bm")
        s_id0 = sem("s_id0")
        s_const = sem("s_const")
        s_rep = sem("s_rep")
        s_wmT_ps = sem("s_wmT_ps")
        s_wmT = sem("s_wmT")
        s_c_ps = sem("s_c_ps")
        s_csq = sem("s_csq")
        s_chi = sem("s_chi")
        s_clo = sem("s_clo")
        s_a_ps = sem("s_a_ps")
        s_asq = sem("s_asq")
        s_ahi = sem("s_ahi")
        s_alo = sem("s_alo")
        s_rows_ps = sem("s_rows_ps")
        s_rows = sem("s_rows")
        s_fro_ps = sem("s_fro_ps")
        s_fro = sem("s_fro")
        s_root = sem("s_root")
        s_wscale = sem("s_wscale")
        s_dve = sem("s_dve")
        s_val = [sem(f"s_val{i}") for i in range(2)]
        s_key = [sem(f"s_key{i}") for i in range(2)]
        s_xs = [sem(f"s_xs{i}") for i in range(2)]
        s_vtop = sem("s_vtop")
        s_vs = [sem(f"s_vs{i}") for i in range(4)]
        s_vscale = sem("s_vscale")
        s_vphi = sem("s_vphi")
        s_vplo = sem("s_vplo")
        s_vT = [sem(f"s_vT{i}") for i in range(2)]
        s_vmm = sem("s_vmm")
        s_v = sem("s_v")
        s_ksq = sem("s_ksq")
        s_stat = sem("s_stat")
        s_kvmax = sem("s_kvmax")
        s_kvT = sem("s_kvT")
        s_kvrow = sem("s_kvrow")
        s_kvall = sem("s_kvall")
        s_bound2 = sem("s_bound2")
        s_scales = sem("s_scales")
        s_var = sem("s_var")
        s_ln = sem("s_ln")
        s_x = [sem(f"s_x{i}") for i in range(2)]
        s_h = sem("s_h")
        s_hhi = sem("s_hhi")
        s_hlo = sem("s_hlo")
        s_hT = [sem(f"s_hT{i}") for i in range(2)]
        s_scrap = sem("s_scrap")
        s_c = sem("s_c")
        s_q_ps = sem("s_q_ps")
        s_q32 = sem("s_q32")
        s_qhi = sem("s_qhi")
        s_qlo = sem("s_qlo")
        s_qout = [sem(f"s_qout{i}") for i in range(2)]
        s_khi = sem("s_khi")
        s_klo = sem("s_klo")
        s_kT = [sem(f"s_kT{i}") for i in range(3)]
        s_vhi = sem("s_vhi")
        s_vlo = sem("s_vlo")
        s_adj = [sem(f"s_adj{i}") for i in range(2)]
        s_qT = [sem(f"s_qT{i}") for i in range(2)]
        s_xrow = [sem(f"s_xrow{i}") for i in range(2)]
        s_xb = sem("s_xb")
        s_ccur = sem("s_ccur")
        s_qk = sem("s_qk")
        s_score = sem("s_score")
        s_times = sem("s_times")
        s_abs = sem("s_abs")
        s_mask = sem("s_mask")
        s_masked = sem("s_masked")
        s_nmax = sem("s_nmax")
        s_exp = sem("s_exp")
        s_phi = sem("s_phi")
        s_plo = sem("s_plo")
        s_pT = [sem(f"s_pT{i}") for i in range(2)]
        s_pv = sem("s_pv")
        s_rd = sem("s_rd")
        s_rden = sem("s_rden")
        s_fin = sem("s_fin")
        s_out = [sem(f"s_out{i}") for i in range(2)]

        x_t = x.rearrange("(t p) d -> t p d", p=P)
        x_s = x.rearrange("(s r p) d -> s p r d", p=P, r=CT)
        x_h = x.rearrange("(g r p) d -> g p r d", p=P, r=2)
        val_s = value.rearrange("(s r p) d -> s p r d", p=P, r=CT)
        adj_t = adj.rearrange("(t p) (h m) -> t h p m", p=P, h=2)
        out_t = out.rearrange("(t p) d -> t p d", p=P)

        def row(view, b):
            if isinstance(b, int):
                return view[b]
            rest = " ".join("bcdef"[:len(view.shape) - 2])
            return view[bass.ds(b, 1)].rearrange(f"o a {rest} -> (o a) {rest}")

        def col(view, b, n=1):
            return view[:, b:b + n] if isinstance(b, int) else view[:, bass.ds(b, n)]

        def tile_of(tensor, t):
            if isinstance(t, int):
                return tensor[:, t, :]
            return tensor[:, bass.ds(t, 1), :].rearrange("p o n -> p (o n)")

        def tiles_of(tensor, t, n):
            return tensor[:, t:t + n, :] if isinstance(t, int) else tensor[:, bass.ds(t, n), :]

        def half_of(tensor, t, h):
            view = tensor[:, :, :].bitcast(fp16)
            if isinstance(t, int):
                return view[:, t, h * D:(h + 1) * D]
            return view[:, bass.ds(t, 1), h * D:(h + 1) * D].rearrange("p o n -> p (o n)")

        def group_phase(eng, group):
            for s in (-2, -1, 0):
                group(s, s % 2)
            with eng.Fori(1, NS - 4, 2) as s:
                group(s, 1)
                group(s + 1, 0)
            for s in (NS - 3, NS - 2, NS - 1):
                group(s, s % 2)

        FIRST = NS // 2 - 1

        def key_use(g):
            if g <= FIRST:
                return 0, g
            return ((1, 0), (0, FIRST + 1), (2, 0), (1, 1))[g - FIRST - 1]

        def key_at(s, par, f):
            if not isinstance(s, int):
                return (s * (CT // 2), s) if par == 0 and f == 0 else None
            steps = {(2 * g, 0): g for g in range(FIRST)}
            steps.update({(NS - 2, 0): FIRST, (NS - 2, 2): FIRST + 1,
                          (NS - 1, 0): FIRST + 2, (NS - 1, 1): FIRST + 3, (NS - 1, 3): FIRST + 4})
            g = steps.get((s, f))
            return None if g is None else (CT * g, 2 * g)

        def key_place(twice):
            return key_use(twice // 2) if isinstance(twice, int) else (0, None)

        def v_tiles(s, f):
            return [s * (CT - 1) + f - 1] if f and inside(s, NS, 1) else []

        def v_late(b, c):
            first = (CT - 1) * (NS - 1)
            if not early(b, 2):
                return []
            return [t for t in range(first, NT) if (b, c) == (1, 1 + (t - first) * (NC - 1) // (NT - first))]

        def main_phase(eng, block):
            for b in range(4):
                block(b, b % 2)
            with eng.Fori(4, NT - 3, 2) as b:
                block(b, 0)
                block(b + 1, 1)
            for b in range(NT - 2, NT + 2):
                block(b, b % 2)

        def inside(i, count, ahead=0):
            return not isinstance(i, int) or 0 <= i + ahead < count

        def early(i, first):
            return isinstance(i, int) and i < first

        def lagged(b, c, lag):
            back = (lag - c + NC - 1) // NC if lag > c else 0
            blk, chunk = b - back, c - lag + back * NC
            if isinstance(b, int) and not 0 <= blk < NT:
                return None
            return blk, chunk, back

        block_ = ctx.enter_context(nc.Block())

        @block_.sync
        def _(sp):
            sp.dma_start(wm_sb, Wm.rearrange("(t p) n -> p t n", p=P)).then_inc(s_wm, 16)
            sp.dma_start(wv_sb, Wv.rearrange("(t p) n -> p t n", p=P)).then_inc(s_wv, 16)
            for i, b in enumerate((bq, bk)):
                sp.dma_start(b_cols[:, i, :], b.rearrange("(p t) -> p t", p=P)).then_inc(s_b, 16)
            sp.dma_start(b_cols[:, 2, :], bv.rearrange("(t p) -> p t", p=P), allow_slow_non_contiguous=True).then_inc(s_b, 16)
            sp.dma_start(bm_row, bm.rearrange("(o n) -> o n", o=1)).then_inc(s_bm, 16)
            sp.dma_start(wq_sb, Wq.rearrange("(p t) n -> p t n", p=P)).then_inc(s_wq, 16)
            sp.dma_start(wk_sb, Wk.rearrange("(p t) n -> p t n", p=P)).then_inc(s_wk, 16)

            def load_keys(half):
                tiles = slice(half * NT // 2, (half + 1) * NT // 2)
                sp.dma_start(key_sb[:, tiles, :], key.rearrange("(g t p) d -> g p t d", g=2, p=P)[half]
                             ).then_inc(s_key[half], 16)

            load_keys(0)

            def group(s, par):
                if inside(s, NS, 2):
                    if early(s, 0):
                        if s == -2:
                            sp.wait_ge(s_c_ps, DT)
                        else:
                            sp.wait_ge(s_wmT_ps, DT)
                    else:
                        sp.wait_ge(s_vplo, CT * (s + 1))
                    sp.dma_start(rows_in[par], row(val_s, s + 2)).then_inc(s_val[par], 16)
                else:
                    sp.wait_ge(s_vplo, CT * (s + 1))
                    sp.dma_start(rows_in[par], row(x_s, s + 2 - NS)).then_inc(s_x[par], 16)
                if early(s, 0) and s == -1:
                    load_keys(1)
                for half in range(2):
                    if inside(s, NS, 1):
                        if early(s, 0):
                            sp.wait_ge(s_rows_ps, 3)
                        else:
                            sp.wait_ge(s_stat, CT * s + 2 + 2 * half)
                        if not early(s, -1):
                            sp.dma_start(x_stat[half], row(x_h, 2 * (s + 1) + half)).then_inc(s_xs[half], 16)
                for half in range(2):
                    if inside(s, NS, 1) and not early(s, -1):
                        sp.wait_ge(s_vplo, CT * (s + 1) + 2 * half + 2)
                        sp.nop(nofuse=True)
                        if not early(s, 1):
                            sp.wait_ge(s_vmm, CT * s)
                            sp.nop(nofuse=True)
                        sp.dma_start_transpose(
                            rowT[1 - par][:, 2 * half:2 * half + 2].rearrange("p r h d m -> p (r h d) m"),
                            row_pair[:, 2 * half:2 * half + 2].rearrange("p r h n -> p (r h n)")
                        ).then_inc(s_vT[half], 16)

            group_phase(sp, group)

            def load_q(b, par):
                sp.dma_start(qT[:, par].rearrange("p f h n -> p (f h n)"),
                             row(q_scratch, b).rearrange("p f h n -> p (f h n)")).then_inc(s_qT[par], 16)

            def load_adj(b, h):
                sp.dma_start(adj_half[h], row(adj_t[:, h], b)).then_inc(s_adj[h], 16)

            def store_q(s, half):
                sp.wait_ge(s_qlo, DT * s + 2 * half + 2)
                dst = q_scratch.rearrange("(s r) p (g f) h n -> g s p r (f h n)", r=CT, g=2)
                sp.dma_start(row(dst[half], s), q_stage[:, :, 2 * half:2 * half + 2].rearrange("p r f h n -> p r (f h n)")
                             ).then_inc(s_qout[half], 16)

            def transpose_key(tile, twice):
                buf, _ = key_place(twice)
                sp.wait_ge(s_klo, twice + 2)
                sp.nop(nofuse=True)
                sp.dma_start_transpose(
                    tiles_of(key_sb, tile, CT).bitcast(fp16).rearrange("p t (f m) -> p (t f) m", m=P),
                    key_buf[buf].rearrange("p r h n -> p (r h n)")).then_inc(s_kT[buf], 16)

            def group(s, par):
                for half in range(2):
                    if inside(s, NS, 1) and not early(s, -1):
                        sp.wait_ge(s_hlo, 2 * (s + 1) + half + 1)
                        sp.nop(nofuse=True)
                        if early(s, 1):
                            sp.wait_ge(s_vmm, CT * (NS + s))
                        else:
                            sp.wait_ge(s_q_ps, DT * s)
                            sp.nop(nofuse=True)
                        sp.dma_start_transpose(
                            rowT[1 - par][:, 2 * half:2 * half + 2].rearrange("p r h d m -> p (r h d) m"),
                            row_pair[:, 2 * half:2 * half + 2].rearrange("p r h n -> p (r h n)")
                        ).then_inc(s_hT[half], 16)
                if inside(s, NS, 3) and not early(s, -1):
                    sp.wait_ge(s_hlo, 2 * (s + 2))
                    sp.wait_ge(s_c, s + 2)
                    sp.dma_start(rows_in[1 - par], row(x_s, s + 3)).then_inc(s_x[1 - par], 16)
                if inside(s, NS) and not early(s, 1):
                    store_q(s - 1, 1)
                if isinstance(s, int) and s == NS - 1:
                    sp.wait_ge(s_c, NS)
                    sp.wait_ge(s_qout[0], 16)
                    sp.wait_ge(s_qout[1], 16)
                    load_q(0, 0)
                    for half in range(2):
                        sp.wait_ge(s_hT[half], 16 * NS)
                    load_adj(0, 0)
                if inside(s, NS):
                    for f in range(DT):
                        if f == 1:
                            store_q(s, 0)
                        if isinstance(s, int) and (s, f) == (NS - 1, DT - 1):
                            sp.wait_ge(s_kT[0], 16 * (FIRST + 2))
                            load_adj(0, 1)
                        if key_at(s, par, f):
                            transpose_key(*key_at(s, par, f))

            group_phase(sp, group)
            store_q(NS - 1, 1)
            for half in range(2):
                sp.wait_ge(s_qout[half], 16 * NS)

            def block(b, par):
                if inside(b, NT, 1):
                    if not early(b, 1):
                        sp.wait_ge(s_qk, NC * b)
                    load_q(b + 1, 1 - par)
                transpose(b - 1, 0)
                if not early(b, 2):
                    sp.wait_ge(s_fin, b - 1)
                    sp.dma_start(row(out_t, b - 2), x_row[:, par, :]).then_inc(s_out[par], 16)
                transpose(b - 1, 1)
                if inside(b, NT, 1):
                    sp.wait_ge(s_masked, NC * b + 4)
                    load_adj(b + 1, 0)
                transpose(b - 1, 2)
                if inside(b, NT):
                    if not early(b, 2):
                        sp.wait_ge(s_out[par], 8 * (b - par))
                    sp.dma_start(x_row[:, par, :], row(x_t, b)).then_inc(s_xrow[par], 16)
                transpose(b - 1, 3)
                if inside(b, NT, 1):
                    sp.wait_ge(s_masked, NC * b + 8)
                    load_adj(b + 1, 1)

            def transpose(b, j):
                if not inside(b, NT):
                    return
                sp.wait_ge(s_plo, PAIRS * b + j + 1)
                sp.nop(nofuse=True)
                if not (early(b, 1) and j < 2):
                    sp.wait_ge(s_pv, NC * b + 2 * j - 2)
                    sp.nop(nofuse=True)
                sp.dma_start_transpose(pT[j % 2].rearrange("p h k n -> p (h k) n"), p_pair[j % 2]
                                       ).then_inc(s_pT[j % 2], 16)

            main_phase(sp, block)
            for par in range(2):
                sp.wait_ge(s_out[par], 16 * (NT // 2))

        @block_.gpsimd
        def _(gp):
            nc.gpsimd.memset(ident[:, :], 0.0).then_inc(s_id0, 1)
            nc.gpsimd.memset(ones[:, :], 1.0).then_inc(s_const, 1)
            gp.wait_ge(s_id0, 1)
            nc.gpsimd.affine_select(out=ident[:, :], in_=ident[:, :], compare_op=ALU.not_equal, fill=1.0,
                                    base=0, pattern=[[-1, P]], channel_multiplier=1).then_inc(s_const, 1)
            def group(s, par):
                for f in range(DT):
                    if inside(s, NS):
                        gp.wait_ge(s_qhi, DT * s + f + 1)
                        nc.gpsimd.tensor_tensor(q_stage[:, :, f, 1, :],
                                                qT_f32[:, f % 2, :].rearrange("p (r n) -> p r n", r=CT),
                                                q_stage[:, :, f, 0, :], ALU.subtract).then_inc(s_qlo, 1)
                    half = f
                    if inside(s, NS, 2) and 0 <= half < 2:
                        gp.wait_ge(s_h, CT * (s + 2) + 2 * half + 2)
                        if early(s, -1):
                            gp.wait_ge(s_vT[half], 16 * NS)
                        else:
                            gp.wait_ge(s_hT[half], 16 * (s + 2))
                        gp.nop(nofuse=True)
                        nc.gpsimd.tensor_scalar(row_pair[:, 2 * half:2 * half + 2, 0, :],
                                                rows_in[par][:, 2 * half:2 * half + 2, :], HSCALE, 1.0,
                                                ALU.mult, ALU.mult).then_inc(s_hhi, 1)

            group_phase(gp, group)

            def block(b, par):
                if isinstance(b, int) and b >= NT:
                    return
                gp.wait_ge(s_xrow[par], 16 * (b // 2 + 1) if isinstance(b, int) else 8 * (b - par) + 16)
                nc.gpsimd.tensor_tensor(x_row[:, par, :], x_row[:, par, :], out_bias[:, :],
                                        ALU.add).then_inc(s_xb, 1)

            main_phase(gp, block)

        @block_.tensor
        def _(pe):
            pe.wait_ge(s_const, 2)
            pe.wait_ge(s_wm, 16)
            for i in range(DT):
                for j in range(DT):
                    last = nc.tensor.transpose(bank[i][:, j * P:(j + 1) * P], wm_sb[:, j, i * P:(i + 1) * P],
                                               ident[:, :])
                last.then_inc(s_wmT_ps, 1)
            pe.wait_ge(s_wv, 16)
            pe.wait_ge(s_wmT, DT)
            for d in range(DT):
                for i in range(DT):
                    last = nc.tensor.matmul(bank[4 + d][:, :], wv_sb[:, i, d * P:(d + 1) * P], wmT[:, i, :],
                                            start=(i == 0), stop=(i == DT - 1))
                last.then_inc(s_c_ps, 1)
            pe.wait_ge(s_rep, 3)
            pe.wait_ge(s_bm, 16)
            for i in range(DT):
                nc.tensor.matmul(bank[0][:, :], b_rep[:, 2, i, :], wmT[:, i, :], start=(i == 0), stop=False)
            nc.tensor.matmul(bank[0][:, :], ones[0:1, :], bm_row, start=False, stop=True).then_inc(s_rows_ps, 1)
            pe.wait_ge(s_csq, DT)
            nc.tensor.matmul(bank[3][:, 0:DT], ones[:, :], sq_sums[:, 0, :], start=True, stop=True).then_inc(s_fro_ps, 1)
            pe.wait_ge(s_wq, 16)
            for j in range(DT):
                last = nc.tensor.matmul(bank[1][:, :], b_rep[:, 1, j, :], wq_sb[:, j, :],
                                        start=(j == 0), stop=(j == DT - 1))
            last.then_inc(s_rows_ps, 1)
            pe.wait_ge(s_wk, 16)
            for f in range(DT):
                for j in range(DT):
                    nc.tensor.matmul(bank[2][:, f:f + 1], wk_sb[:, j, f * P:(f + 1) * P], b_cols[:, 0, j:j + 1],
                                     start=(j == 0), stop=(j == DT - 1))
            for j in range(DT):
                last = nc.tensor.matmul(bank[2][:, DT:DT + 1], b_rep[:, 0, j, :], b_cols[:, 1, j:j + 1],
                                        start=(j == 0), stop=(j == DT - 1))
            last.then_inc(s_rows_ps, 1)
            for e in range(DT):
                if e < 3:
                    pe.wait_ge(s_rows, (1, 2, 4)[e])
                else:
                    pe.wait_ge(s_fro, 1)
                for j in range(DT):
                    last = nc.tensor.matmul(bank[e][:, :], wq_sb[:, j, e * P:(e + 1) * P], wk_sb[:, j, :],
                                            start=(j == 0), stop=(j == DT - 1))
                last.then_inc(s_a_ps, 1)
            pe.wait_ge(s_clo, DT)
            pe.wait_ge(s_rows, 5)
            pe.wait_ge(s_asq, DT)
            nc.tensor.matmul(bank[7][:, 0:2 * DT], ones[:, :], sq_sums[:, 1:3, :].rearrange("p i f -> p (i f)"),
                             start=True, stop=True).then_inc(s_fro_ps, 1)

            THREE = ((0, 0), (0, 1), (1, 0))

            def group(s, par):
                if not inside(s, NS):
                    return
                for r in range(CT):
                    if r % 2 == 0:
                        pe.wait_ge(s_vT[r // 2], 16 * (s + 1))
                    if not early(s, 1):
                        pe.wait_ge(s_v, CT * (s - 1) + r + 1)
                    elif r == 3:
                        pe.wait_ge(s_fro, 2)
                    for i, (d, hv, hc) in enumerate([(d, *hh) for d in range(DT) for hh in THREE]):
                        last = nc.tensor.matmul(bank[4 + r][:, :], rowT[par][:, r, hv, d, :], c_pair[:, d, hc, :],
                                                start=(i == 0), stop=(i == 3 * DT - 1))
                    last.then_inc(s_vmm, 1)
                    if isinstance(s, int) and s == NS - 1:
                        if r == 2:
                            pe.wait_ge(s_kvmax, 1)
                            pe.wait_ge(s_alo, DT)
                            for i in range(2):
                                last = nc.tensor.matmul(bank[0][0:1, i * P:(i + 1) * P], kv_max[:, i:i + 1],
                                                        ident[:, :], start=True, stop=True)
                            last.then_inc(s_kvT, 1)
                        if r == 3:
                            pe.wait_ge(s_kvrow, 1)
                            nc.tensor.matmul(bank[0][:, 0:2], ones[0:1, :], kv_row[:, :], start=True,
                                             stop=True).then_inc(s_kvall, 1)

            group_phase(pe, group)

            def group(s, par):
                if not inside(s, NS):
                    return
                for half in range(2):
                    pe.wait_ge(s_hT[half], 16 * (s + 1))
                for f in range(DT):
                    if early(s, 1):
                        pe.wait_ge(s_v, CT * (NS - 1) + f + 1)
                    else:
                        pe.wait_ge(s_q32, DT * (s - 1) + f + 1)
                    for i, (e, hh, ha) in enumerate([(e, *hh) for e in range(DT) for hh in THREE]):
                        last = nc.tensor.matmul(bank[4 + f][:, :], a_pair[:, e, ha, f * P:(f + 1) * P],
                                                rowT[par][:, :, hh, e, :], start=(i == 0), stop=(i == 3 * DT - 1))
                    last.then_inc(s_q_ps, 1)

            group_phase(pe, group)

            def block(b, par):
                for c in range(NC):
                    if not (isinstance(b, int) and b >= NT):
                        if c == 0:
                            pe.wait_ge(s_qT[par], 16 * (b // 2 + 1) if isinstance(b, int) else 8 * (b - par) + 16)
                        if early(b, 1):
                            buf, before = key_use(c)
                            pe.wait_ge(s_kT[buf], 16 * (before + 1))
                            if c == 0:
                                pe.wait_ge(s_kvall, 1)
                        if not (isinstance(b, int) and b == 0 and c < 4):
                            pe.wait_ge(s_score, NC * b + c - 3)
                        for i, (f, hq, hk) in enumerate([(f, *hh) for f in range(DT) for hh in THREE]):
                            last = nc.tensor.matmul(bank[c % 4][:, :], qT[:, par, f, hq, :],
                                                    k16[:, c * CT:(c + 1) * CT, hk, f, :],
                                                    start=(i == 0), stop=(i == 3 * DT - 1))
                        last.then_inc(s_qk, 1)
                    at = lagged(b, c, VLAG)
                    if at:
                        vb, vc, back = at
                        j = vc // 2
                        if vc % 2 == 0:
                            pe.wait_ge(s_pT[j % 2], 16 * (2 * vb + j // 2 + 1))
                        if isinstance(vb, int) and vb == 0:
                            pe.wait_ge(s_vlo, CT * (vc + 1))
                            if vc == 0:
                                pe.wait_ge(s_q32, NT)
                        if vc == 0 and not (isinstance(vb, int) and vb < 2):
                            pe.wait_ge(s_fin, vb - 1)
                        o = bank[6 + (par + back) % 2]
                        for k in range(CT):
                            m = vc * CT + k
                            for i, (hp, hv) in enumerate(THREE):
                                last = nc.tensor.matmul(o[:, :], pT[j % 2][:, hp, vc % 2 * CT + k, :], v16[:, m, hv, :],
                                                        start=(m == 0 and i == 0), stop=(m == NT - 1 and i == 2))
                        last.then_inc(s_pv, 1)

            main_phase(pe, block)

        @block_.scalar
        def _(act):
            for i in range(DT):
                act.wait_ge(s_wmT_ps, i + 1)
                nc.scalar.activation(wmT[:, i, :], bank[i][:, :], ACT.Copy).then_inc(s_wmT, 1)

            def split_weights(first, pair, which, ready, squared, scales, hi):
                for i in range(DT):
                    act.wait_ge(ready, i + 1)
                    if which or i:
                        act.wait_ge(squared if i else s_csq, i if i else DT)
                    nc.scalar.activation(squares[:, :], bank[first + i][:, :], ACT.Square,
                                         accum_out=sq_sums[:, which, i:i + 1]).then_inc(squared, 1)
                act.wait_ge(s_fro, which + 1)
                nc.scalar.activation(scales[:, 0:1], fro_sq[:, which:which + 1], ACT.Sqrt).then_inc(s_root, 1)
                act.wait_ge(s_wscale, which + 1)
                for i in range(DT):
                    nc.scalar.activation(pair[:, i, 0, :], bank[first + i][:, :], ACT.Copy,
                                         scale=scales[:, 3:4]).then_inc(hi, 1)

            split_weights(4, c_pair, 0, s_c_ps, s_csq, sc_c, s_chi)

            def relu(s, par, r):
                if r == 0:
                    act.wait_ge(s_x[par], 8 * (s - par) + 16)
                t = CT * s + r
                nc.scalar.activation(rows_in[par][:, r, :], rows_in[par][:, r, :], ACT.Relu,
                                     scale=col(ln_scale, t), bias=col(ln_bias, t)).then_inc(s_h, 1)

            def group(s, par):
                for r in range(CT):
                    if inside(s, NS, 1) and not early(s, -1):
                        if r == 0:
                            act.wait_ge(s_vscale, s + 2)
                            if early(s, 0):
                                act.wait_ge(s_rows_ps, 3)
                        if not early(s, 0) and r % 2 == 0:
                            act.wait_ge(s_vT[r // 2], 16 * (s + 1))
                        nc.scalar.activation(row_pair[:, r, 0, :], rows_in[1 - par][:, r, :], ACT.Copy,
                                             scale=val_scale[:, 1 - par, r:r + 1]).then_inc(s_vphi, 1)
                if isinstance(s, int) and s == 0:
                    split_weights(0, a_pair, 1, s_a_ps, s_asq, sc_a, s_ahi)
                if isinstance(s, int) and s == NS - 1:
                    act.wait_ge(s_var, 1)
                    nc.scalar.activation(ln_root[:, :], ln_v[:, :], ACT.Sqrt).then_inc(s_root, 1)
                    act.wait_ge(s_ln, 1)
                    for r in range(CT):
                        relu(0, 0, r)
                for r in range(CT):
                    if inside(s, NS):
                        if r == 0 and early(s, 1):
                            for half in range(2):
                                act.wait_ge(s_key[half], 16)
                        if not (early(s, 1) and r == 0):
                            act.wait_ge(s_ksq, CT * s + r)
                        nc.scalar.activation(squares[:, :], tile_of(key_sb, CT * s + r), ACT.Square,
                                             accum_out=col(key_sq, CT * s + r)).then_inc(s_ksq, 1)
                for r in range(CT):
                    if inside(s, NS):
                        act.wait_ge(s_vmm, CT * s + r + 1)
                        nc.scalar.activation(tile_of(v_sb, CT * s + r + 1), bank[4 + r][:, :], ACT.Copy,
                                             scale=col(val_undo, CT * s + r)).then_inc(s_v, 1)
                        if isinstance(s, int) and s == NS - 1:
                            relu(1, 1, r)

            group_phase(act, group)

            act.wait_ge(s_bound2, 1)
            nc.scalar.activation(sc3[:, 0, :], bound_sq[:, :], ACT.Sqrt).then_inc(s_root, 1)
            act.wait_ge(s_scales, 1)

            def group(s, par):
                if inside(s, NS):
                    for f in range(DT):
                        if key_at(s, par, f):
                            key_hi(*key_at(s, par, f))
                        if inside(s, NS, 2) and f < 2:
                            for r in (2 * f, 2 * f + 1):
                                relu(s + 2, par, r)
                        act.wait_ge(s_q_ps, DT * s + f + 1)
                        if not (early(s, 1) and f < 2):
                            act.wait_ge(s_qlo, DT * s + f - 1)
                        nc.scalar.activation(qT_f32[:, f % 2, :], bank[4 + f][:, :], ACT.Identity,
                                             scale=q_undo[:, 0:1], bias=q_bias[:, f:f + 1]).then_inc(s_q32, 1)
                        for t in v_tiles(s, f):
                            split_v(t)

            def key_hi(tile, twice):
                buf, before = key_place(twice)
                if not isinstance(twice, int):
                    act.wait_ge(s_kT[0], 8 * twice)
                elif before:
                    act.wait_ge(s_kT[buf], 16 * before)
                elif buf == 0:
                    act.wait_ge(s_vmm, NT)
                else:
                    act.wait_ge(s_hlo, 2 * (NS - 2 + buf))
                    act.wait_ge(s_c, NS - 2 + buf)
                nc.scalar.activation(key_buf[buf][:, :, 0, :], tiles_of(key_sb, tile, CT), ACT.Copy,
                                     scale=sc3[:, 3, 0:1]).then_inc(s_khi, 2)

            def split_v(t):
                if not early(t, 1):
                    act.wait_ge(s_vlo, t)
                nc.scalar.activation(half_of(v_sb, t, 0), tile_of(v_sb, t + 1), ACT.Copy,
                                     scale=sc3[:, 3, 1:2]).then_inc(s_vhi, 1)

            group_phase(act, group)
            nc.scalar.activation(sc_a[:, 0:1], ones[:, 0:1], ACT.Exp)
            act.wait_ge(s_q_ps, NT)
            act.wait_ge(s_hlo, 2 * NS)
            act.wait_ge(s_c, NS)

            def block(b, par):
                for c in range(NC):
                    if not (isinstance(b, int) and b >= NT):
                        act.wait_ge(s_qk, NC * b + c + 1)
                        if c == 0:
                            act.wait_ge(s_ccur, b + 1)
                            if early(b, 2) and b == 1:
                                act.wait_ge(s_kT[1], 32)
                                act.wait_ge(s_kT[2], 16)
                        if not early(b, 2) and c % 2 == 0:
                            act.wait_ge(s_plo, PAIRS * (b - 2) + c // 2 + 1)
                        nc.scalar.activation(probs[par][:, c * 512:(c + 1) * 512], bank[c % 4][:, :], ACT.Identity,
                                             scale=inv_qk[:, 0:1], bias=c_cur[:, par:par + 1]).then_inc(s_score, 1)
                    if c == 0 and not (isinstance(b, int) and not 0 < b <= NT):
                        act.wait_ge(s_nmax, b)
                        if not (isinstance(b, int) and b < 3):
                            act.wait_ge(s_rd, b - 2)
                        nc.scalar.activation(probs[1 - par], probs[1 - par], ACT.Exp,
                                             bias=neg_max[:, 1 - par:2 - par], scale=1.0,
                                             accum_out=den[:, 1 - par:2 - par]).then_inc(s_exp, 1)
                    if (c == 0 or c % 2 == 1 and c > 1) and inside(b, NT, -1):
                        j = c // 2
                        if j == 0:
                            act.wait_ge(s_exp, b)
                        if not (early(b, 2) and j < 2):
                            act.wait_ge(s_pT[j % 2], 16 * (2 * (b - 1) + j // 2))
                        nc.scalar.activation(p_pair[j % 2][:, 0:1024], probs[1 - par][:, j * 1024:(j + 1) * 1024],
                                             ACT.Copy, scale=PSCALE).then_inc(s_phi, 1)
                    for t in v_late(b, c):
                        split_v(t)
                    if not (isinstance(b, int) and b >= NT):
                        act.wait_ge(s_times, NC * b + c + 1)
                        nc.scalar.activation(adj_half[c // 4][:, (c % 4) * 512:(c % 4 + 1) * 512],
                                             probs[par][:, c * 512:(c + 1) * 512], ACT.Abs).then_inc(s_abs, 1)

            main_phase(act, block)

        @block_.vector
        def _(dve):
            chain = [0]

            def link(ins):
                chain[0] += 1
                ins.then_inc(s_dve, 1)
                dve.wait_ge(s_dve, chain[0])

            dve.wait_ge(s_const, 2)
            dve.wait_ge(s_b, 48)
            for i in range(3):
                for j in range(DT):
                    last = nc.vector.tensor_scalar(b_rep[:, i, j, :], ones[:, :], b_cols[:, i, j:j + 1], None, ALU.mult)
                last.then_inc(s_rep, 1)

            def scales_from(sc, sems=None):
                at = [sc[:, i] for i in range(5)] if len(sc.shape) > 2 else [sc[:, i:i + 1] for i in range(5)]
                link(nc.vector.tensor_scalar(at[0], at[0], 2.0 ** -50, None, ALU.max))
                link(nc.vector.tensor_scalar(at[1].bitcast(i32), at[0].bitcast(i32), 0x7F800000, None,
                                             ALU.bitwise_and))
                link(nc.vector.reciprocal(at[2], at[1]))
                link(nc.vector.tensor_scalar(at[3], at[2], TOP, None, ALU.mult))
                return nc.vector.tensor_scalar(at[4], at[1], 1.0 / TOP, None, ALU.mult)

            dve.wait_ge(s_fro_ps, 1)
            nc.vector.tensor_reduce(fro_sq[:, 0:1], bank[3][:, 0:DT], axis=AX.X, op=ALU.add).then_inc(s_fro, 1)
            dve.wait_ge(s_root, 1)
            scales_from(sc_c).then_inc(s_wscale, 1)
            for i in range(DT):
                dve.wait_ge(s_chi, i + 1)
                nc.vector.scalar_tensor_tensor(c_pair[:, i, 1, :], bank[4 + i][:, :], sc_c[:, 3:4], c_pair[:, i, 0, :],
                                               ALU.mult, ALU.subtract).then_inc(s_clo, 1)
            dve.wait_ge(s_rows_ps, 1)
            nc.vector.tensor_copy(out_bias[:, :], bank[0][:, :]).then_inc(s_rows, 1)
            dve.wait_ge(s_rows_ps, 2)
            nc.vector.tensor_copy(wq_bk[:, :], bank[1][:, :]).then_inc(s_rows, 1)
            dve.wait_ge(s_rows_ps, 3)
            nc.vector.tensor_copy(q_bias[:, :], bank[2][:, 0:DT]).then_inc(s_rows, 1)
            nc.vector.tensor_copy(bq_bk[:, :], bank[2][:, DT:DT + 1]).then_inc(s_rows, 1)
            dve.wait_ge(s_rows, 4)
            nc.vector.tensor_tensor(sq_sums[:, 2, :], q_bias[:, :], q_bias[:, :], ALU.mult).then_inc(s_rows, 1)

            def tops(s, par):
                dve.wait_ge(s_val[par], 8 * (s + 2 - par) + 16)
                nc.vector.tensor_reduce(col(val_top, CT * (s + 2), CT), rows_in[par], axis=AX.X, op=ALU.max,
                                        apply_absolute_value=True).then_inc(s_vtop, 1)
                dve.wait_ge(s_vtop, s + 3)
                at = [val_steps[:, i] for i in range(3)]
                nc.vector.tensor_scalar(at[0], col(val_top, CT * (s + 2), CT), 2.0 ** -50, None,
                                        ALU.max).then_inc(s_vs[0], 1)
                dve.wait_ge(s_vs[0], s + 3)
                nc.vector.tensor_scalar(at[1].bitcast(i32), at[0].bitcast(i32), 0x7F800000, None,
                                        ALU.bitwise_and).then_inc(s_vs[1], 1)
                dve.wait_ge(s_vs[1], s + 3)
                nc.vector.reciprocal(at[2], at[1]).then_inc(s_vs[2], 1)
                dve.wait_ge(s_vs[2], s + 3)
                nc.vector.tensor_scalar(val_scale[:, par], at[2], TOP, None, ALU.mult).then_inc(s_vs[3], 1)
                dve.wait_ge(s_vs[3], s + 3)
                nc.vector.tensor_scalar(col(val_undo, CT * (s + 2), CT), at[1], sc_c[:, 4:5], 1.0 / TOP,
                                        ALU.mult, ALU.mult).then_inc(s_vscale, 1)
                dve.wait_ge(s_vscale, s + 3)

            def layernorm_scales():
                dve.wait_ge(s_stat, NT)
                mean_e, mean_o, m2_e, m2_o = (stats[:, :, i] for i in (1, 4, 2, 5))
                link(nc.vector.tensor_tensor(ln_t[:, 0, :], mean_e, mean_o, ALU.subtract))
                link(nc.vector.tensor_tensor(ln_t[:, 1, :], m2_e, m2_o, ALU.add))
                link(nc.vector.tensor_tensor(ln_t[:, 2, :], ln_t[:, 0, :], ln_t[:, 0, :], ALU.mult))
                link(nc.vector.tensor_scalar(ln_t[:, 1, :], ln_t[:, 1, :], 1.0 / D, EPS, ALU.mult, ALU.add))
                nc.vector.scalar_tensor_tensor(ln_v[:, :], ln_t[:, 2, :], 0.25, ln_t[:, 1, :],
                                               ALU.mult, ALU.add).then_inc(s_var, 1)
                dve.wait_ge(s_root, 3)
                link(nc.vector.reciprocal(ln_scale[:, :], ln_root[:, :]))
                link(nc.vector.tensor_tensor(ln_t[:, 0, :], ln_scale[:, :], ln_scale[:, :], ALU.mult))
                link(nc.vector.tensor_tensor(ln_t[:, 1, :], ln_t[:, 0, :], ln_v[:, :], ALU.mult))
                link(nc.vector.tensor_scalar(ln_t[:, 0, :], ln_t[:, 1, :], -0.5, 1.5, ALU.mult, ALU.add))
                link(nc.vector.tensor_tensor(ln_scale[:, :], ln_scale[:, :], ln_t[:, 0, :], ALU.mult))
                link(nc.vector.tensor_tensor(ln_t[:, 2, :], mean_e, mean_o, ALU.add))
                nc.vector.scalar_tensor_tensor(ln_bias[:, :], ln_t[:, 2, :], -0.5, ln_scale[:, :],
                                               ALU.mult, ALU.mult).then_inc(s_ln, 1)

            def largest():
                dve.wait_ge(s_ksq, NT)
                link(nc.vector.tensor_reduce(kv_max[:, 0:1], key_sq[:, :], axis=AX.X, op=ALU.max))
                nc.vector.tensor_reduce(kv_max[:, 1:2], val_top[:, :], axis=AX.X, op=ALU.max).then_inc(s_kvmax, 1)

            def largest_of_all():
                dve.wait_ge(s_kvT, 1)
                nc.vector.tensor_reduce(kv_row[:, :], bank[0][0:1, 0:2 * P].rearrange("o (i p) -> o i p", i=2),
                                        axis=AX.X, op=ALU.max).then_inc(s_kvrow, 1)

            def bound_scales():
                dve.wait_ge(s_kvall, 1)
                link(nc.vector.tensor_copy(kv_all[:, :], bank[0][:, 0:2]))
                link(nc.vector.tensor_copy(bound_sq[:, 0:1], kv_all[:, 0:1]))
                link(nc.vector.tensor_tensor(bound_sq[:, 1:2], kv_all[:, 1:2], kv_all[:, 1:2], ALU.mult))
                link(nc.vector.tensor_scalar(bound_sq[:, 1:2], bound_sq[:, 1:2], fro_sq[:, 0:1], float(D), ALU.mult, ALU.mult))
                link(nc.vector.scalar_tensor_tensor(bound_sq[:, 2:3], fro_sq[:, 1:2], float(D), fro_sq[:, 2:3],
                                                    ALU.mult, ALU.add))
                link(nc.vector.tensor_scalar(bound_sq[:, 2:3], bound_sq[:, 2:3], 2.0, None, ALU.mult))
                nc.vector.tensor_scalar(bound_sq[:, :], bound_sq[:, :], 1e-30, None, ALU.max).then_inc(s_bound2, 1)
                dve.wait_ge(s_root, 4)
                link(scales_from(sc3))
                link(nc.vector.tensor_tensor(inv_qk0[:, :], sc3[:, 4, 0:1], sc3[:, 4, 2:3], ALU.mult))
                link(nc.vector.tensor_scalar(inv_qk[:, :], inv_qk0[:, :], INV_ROOT, None, ALU.mult))
                link(nc.vector.tensor_scalar(inv_pv[:, :], sc3[:, 4, 1:2], 1.0 / PSCALE, None, ALU.mult))
                link(nc.vector.tensor_tensor(q_undo[:, 1:2], sc_a[:, 4:5], sc3[:, 3, 2:3], ALU.mult))
                link(nc.vector.tensor_scalar(q_undo[:, 0:1], q_undo[:, 1:2], 1.0 / HSCALE, None, ALU.mult))
                nc.vector.tensor_scalar(q_bias[:, :], q_bias[:, :], sc3[:, 3, 2:3], None, ALU.mult).then_inc(s_scales, 1)

            def group(s, par):
                for r in range(CT):
                    if inside(s, NS, 1) and not early(s, -1):
                        dve.wait_ge(s_vphi, CT * (s + 1) + r + 1)
                        nc.vector.scalar_tensor_tensor(row_pair[:, r, 1, :], rows_in[1 - par][:, r, :],
                                                       val_scale[:, 1 - par, r:r + 1], row_pair[:, r, 0, :],
                                                       ALU.mult, ALU.subtract).then_inc(s_vplo, 1)
                if isinstance(s, int) and s == 0:
                    dve.wait_ge(s_fro_ps, 2)
                    nc.vector.tensor_reduce(fro_sq[:, 1:3], bank[7][:, 0:2 * DT].rearrange("p (i f) -> p i f", i=2),
                                            axis=AX.X, op=ALU.add).then_inc(s_fro, 1)
                    dve.wait_ge(s_root, 2)
                    scales_from(sc_a).then_inc(s_wscale, 1)
                    for i in range(DT):
                        dve.wait_ge(s_ahi, i + 1)
                        nc.vector.scalar_tensor_tensor(a_pair[:, i, 1, :], bank[i][:, :], sc_a[:, 3:4],
                                                       a_pair[:, i, 0, :], ALU.mult, ALU.subtract).then_inc(s_alo, 1)
                if inside(s, NS, 2):
                    tops(s, par)
                if inside(s, NS, 1) and not early(s, -1):
                    for r in range(CT):
                        if r % 2 == 0:
                            dve.wait_ge(s_xs[r // 2], 16 * (s + 2))
                        nc.vector.bn_stats(tile_of(stats, CT * (s + 1) + r), x_stat[r // 2][:, r % 2, :]).then_inc(s_stat, 1)

            def h_lo(s, par, half):
                two = slice(2 * half, 2 * half + 2)
                dve.wait_ge(s_hhi, 2 * s + half + 1)
                nc.vector.scalar_tensor_tensor(row_pair[:, two, 1, :], rows_in[par][:, two, :], HSCALE,
                                               row_pair[:, two, 0, :], ALU.mult, ALU.subtract).then_inc(s_hlo, 1)

            def h_dot(s, par, r):
                dve.wait_ge(s_h, CT * s + r + 1)
                if not (early(s, 1) and r == 0):
                    dve.wait_ge(s_scrap, CT * s + r)
                nc.vector.tensor_tensor_reduce(out=scrap[:, :], in0=rows_in[par][:, r, :], in1=wq_bk[:, :],
                                               scale=1.0, scalar=0.0, op0=ALU.mult, op1=ALU.add,
                                               accum_out=c_raw[:, par, r:r + 1]).then_inc(s_scrap, 1)
                if r == CT - 1:
                    dve.wait_ge(s_scrap, CT * (s + 1))
                    nc.vector.tensor_scalar(col(c_all, CT * s, CT), c_raw[:, par, :], bq_bk[:, 0:1], INV_ROOT,
                                            ALU.add, ALU.mult).then_inc(s_c, 1)

            group_phase(dve, group)
            layernorm_scales()
            for half in range(2):
                h_lo(0, 0, half)
            largest()
            largest_of_all()
            for r in range(CT):
                h_dot(0, 0, r)
            bound_scales()
            for half in range(2):
                h_lo(1, 1, half)
            for r in range(CT):
                h_dot(1, 1, r)

            def group(s, par):
                for f in range(DT):
                    if inside(s, NS) and key_at(s, par, f):
                        key_lo(*key_at(s, par, f))
                    if inside(s, NS, 2) and not early(s, 0) and f < 2:
                        for r in (2 * f, 2 * f + 1):
                            h_dot(s + 2, par, r)
                    if inside(s, NS):
                        dve.wait_ge(s_q32, DT * s + f + 1)
                        if f % 2 == 0 and not early(s, 1):
                            dve.wait_ge(s_qout[f // 2], 16 * s)
                        nc.vector.tensor_copy(q_stage[:, :, f, 0, :],
                                              qT_f32[:, f % 2, :].rearrange("p (r n) -> p r n", r=CT)).then_inc(s_qhi, 1)
                    if inside(s, NS, 2) and not early(s, 0) and 1 <= f < 3:
                        h_lo(s + 2, par, f - 1)
                    if inside(s, NS):
                        for t in v_tiles(s, f):
                            split_v(t)
            def key_lo(tile, twice):
                pair = key_buf[key_place(twice)[0]]
                dve.wait_ge(s_khi, twice + 2)
                nc.vector.scalar_tensor_tensor(pair[:, :, 1, :], tiles_of(key_sb, tile, CT), sc3[:, 3, 0:1],
                                               pair[:, :, 0, :], ALU.mult, ALU.subtract).then_inc(s_klo, 2)

            def split_v(t):
                dve.wait_ge(s_vhi, t + 1)
                nc.vector.scalar_tensor_tensor(half_of(v_sb, t, 1), tile_of(v_sb, t + 1), sc3[:, 3, 1:2],
                                               half_of(v_sb, t, 0), ALU.mult, ALU.subtract).then_inc(s_vlo, 1)

            group_phase(dve, group)
            dve.wait_ge(s_c, NS)

            def block(b, par):
                here = inside(b, NT)
                if early(b, 1):
                    nc.vector.tensor_copy(c_cur[:, 0:1], col(c_all, 0)).then_inc(s_ccur, 1)
                for c in range(NC):
                    chunk = probs[par][:, c * 512:(c + 1) * 512]
                    small = adj_half[c // 4][:, (c % 4) * 512:(c % 4 + 1) * 512]
                    if here:
                        if c % 4 == 0:
                            dve.wait_ge(s_adj[c // 4], 16 * (b + 1))
                        dve.wait_ge(s_score, NC * b + c + 1)
                        nc.vector.tensor_tensor(chunk, chunk, small, ALU.mult).then_inc(s_times, 1)
                    if c == 4 and inside(b, NT, 1):
                        nc.vector.tensor_copy(c_cur[:, 1 - par:2 - par], col(c_all, b + 1)).then_inc(s_ccur, 1)
                    if (c == 0 or c % 2 == 1 and c > 1) and inside(b, NT, -1):
                        j = c // 2
                        dve.wait_ge(s_phi, PAIRS * (b - 1) + j + 1)
                        nc.vector.scalar_tensor_tensor(p_pair[j % 2][:, 1024:2048],
                                                       probs[1 - par][:, j * 1024:(j + 1) * 1024], PSCALE,
                                                       p_pair[j % 2][:, 0:1024],
                                                       ALU.mult, ALU.subtract).then_inc(s_plo, 1)
                    for t in v_late(b, c):
                        split_v(t)
                    if here:
                        dve.wait_ge(s_abs, NC * b + c + 1)
                        nc.vector.tensor_scalar(small, small, LIMIT, MASKED, ALU.is_lt, ALU.mult).then_inc(s_mask, 1)
                        dve.wait_ge(s_mask, NC * b + c + 1)
                        dve.nop(nofuse=True)
                        nc.vector.tensor_tensor_reduce(out=chunk, in0=chunk, in1=small, scale=1.0, scalar=-3.0e38,
                                                       op0=ALU.add, op1=ALU.max,
                                                       accum_out=chunk_max[:, c:c + 1]).then_inc(s_masked, 1)
                    if c == (VLAG + NC - 1) % NC + 1:
                        ob = b - 2
                        if not isinstance(b, int) or 0 <= ob < NT:
                            finish(ob, par)
                if here:
                    dve.wait_ge(s_masked, NC * (b + 1))
                    nc.vector.tensor_reduce(neg_max[:, par:par + 1], chunk_max[:, :], axis=AX.X, op=ALU.max,
                                            negate=True).then_inc(s_nmax, 1)

            def finish(b, par):
                dve.wait_ge(s_exp, b + 1)
                nc.vector.reciprocal(rden[:, par:par + 1], den[:, par:par + 1]).then_inc(s_rd, 1)
                dve.wait_ge(s_rd, b + 1)
                nc.vector.tensor_scalar(rden[:, par:par + 1], rden[:, par:par + 1], inv_pv[:, 0:1], None,
                                        ALU.mult).then_inc(s_rden, 1)
                dve.wait_ge(s_rden, b + 1)
                dve.wait_ge(s_pv, NC * (b + 1))
                dve.wait_ge(s_xb, b + 1)
                nc.vector.scalar_tensor_tensor(x_row[:, par, :], bank[6 + par][:, :], rden[:, par:par + 1],
                                               x_row[:, par, :], ALU.mult, ALU.add).then_inc(s_fin, 1)

            main_phase(dve, block)


_INS = ['x', 'adj', 'L0_gnn_key', 'L0_gnn_value', 'L0_gnn_Wq', 'L0_gnn_bq', 'L0_gnn_Wk', 'L0_gnn_bk',
        'L0_gnn_Wv', 'L0_gnn_bv', 'L0_gnn_Wm', 'L0_gnn_bm']
_OUTS = [((4096, 512), 'float32')]


def kernel(**inputs):
    import numpy as _np
    import concourse.bacc as _bacc
    from concourse import mybir as _mybir
    from concourse.bass_utils import run_bass_kernel_spmd as _run

    nc = _bacc.Bacc("TRN2", target_bir_lowering=False, num_devices=1)
    arrays, args = {}, []
    for name in _INS:
        a = _np.ascontiguousarray(inputs[name])
        arrays[f"in_{name}_dram"] = a
        args.append(nc.dram_tensor(f"in_{name}_dram", a.shape, _mybir.dt.from_np(a.dtype), kind="ExternalInput").ap())
    for i, (shape, dtype) in enumerate(_OUTS):
        dt = _mybir.dt.from_np(_np.dtype(dtype))
        args.append(nc.dram_tensor(f"out_{i}_dram", shape, dt, kind="ExternalOutput").ap())
    adjacency_attention(nc, *args)
    r = _run(nc, [arrays], core_ids=[0])
    got = tuple(r.results[0][f"out_{i}_dram"] for i in range(len(_OUTS)))
    return got[0]
```
